# Optimizing a Trainium2 kernel written in Bass

```python
import numpy as np
import jax
import jax.numpy as jnp

def _softmax(x, axis=-1):
    return jax.nn.softmax(x, axis=axis)

def _gelu(x):
    return jax.nn.gelu(x, approximate=True)

def _silu(x):
    return jax.nn.silu(x)

def _sigmoid(x):
    return jax.nn.sigmoid(x)

def _layernorm(x, axis=-1, eps=1e-05):
    m = jnp.mean(x, axis=axis, keepdims=True)
    v = jnp.var(x, axis=axis, keepdims=True)
    return (x - m) / jnp.sqrt(v + eps)

def _scatter_add(tgt, idx, src, axis=0):
    return tgt.at[idx].add(src)

def _segment_sum(src, seg, n):
    return jax.ops.segment_sum(src, seg, n)
kernel_name = 'mk_macaron_d2_jaxref_r4_8c5c6d'

def setup_inputs(seed: int=0):
    np.random.seed(seed)
    _w = jnp.asarray

    def _L0_attn_setup():
        import jax, jax.numpy as jnp
        import numpy as np
        B, M, D, H = (2, 512, 256, 16)

        def _rope(x):
            b, m, d = x.shape
            i = jnp.arange(d // 2, dtype=jnp.float32)
            theta = 10000.0 ** (-2.0 * (i - 1.0) / d)
            ang = jnp.arange(m, dtype=jnp.float32)[:, None] * theta[None, :]
            c, s = (jnp.cos(ang), jnp.sin(ang))
            xe, xo = (x[..., 0::2], x[..., 1::2])
            ye = xe * c + xo * s
            yo = -xe * s + xo * c
            return jnp.stack([ye, yo], axis=-1).reshape(b, m, d)
        key = jax.random.key(seed)
        ks = jax.random.split(key, 8)
        w = lambda k, shape: jax.random.normal(k, shape, jnp.float32) * 0.02
        return {'x': jax.random.normal(ks[0], (B, M, D), jnp.float32), 'wq': w(ks[1], (D, D)), 'wk': w(ks[2], (D, D)), 'wv': w(ks[3], (D, D)), 'in_proj_w': w(ks[4], (3 * D, D)), 'in_proj_b': w(ks[5], (3 * D,)), 'out_w': w(ks[6], (D, D)), 'out_b': w(ks[7], (D,))}
    _L0_attn_in = _L0_attn_setup()

    def _L0_ffn_setup():
        import jax, jax.numpy as jnp
        import numpy as np
        B, L, H, E, FF, C = (4, 512, 256, 8, 1024, 2)
        key = jax.random.key(seed)
        ks = jax.random.split(key, 6)
        s = 0.02
        return {'x': jax.random.normal(ks[0], (B, L, H), dtype=jnp.float32), 'Wg': jax.random.normal(ks[1], (H, E), dtype=jnp.float32) * s, 'W1': jax.random.normal(ks[2], (E, H, FF), dtype=jnp.float32) * s, 'b1': jnp.zeros((E, FF), dtype=jnp.float32), 'W2': jax.random.normal(ks[3], (E, FF, H), dtype=jnp.float32) * s, 'b2': jnp.zeros((E, H), dtype=jnp.float32)}
    _L0_ffn_in = _L0_ffn_setup()

    def _L1_attn_setup():
        import jax, jax.numpy as jnp
        import numpy as np
        D_K, D_MODEL, NUM_HEADS = (64, 256, 16)

        def _xavier(key, shape):
            fan_in, fan_out = (shape[-2], shape[-1])
            limit = float(np.sqrt(6.0 / (fan_in + fan_out)))
            return jax.random.uniform(key, shape, jnp.float32, -limit, limit)
        key = jax.random.key(seed)
        kx, kq, kk, kv, ko = jax.random.split(key, 5)
        x = jax.random.normal(kx, (2, 512, D_MODEL), dtype=jnp.float32)
        w_q = _xavier(kq, (NUM_HEADS, D_MODEL, D_K))
        w_k = _xavier(kk, (NUM_HEADS, D_MODEL, D_K))
        w_v = _xavier(kv, (NUM_HEADS, D_MODEL, D_K))
        w_o = _xavier(ko, (NUM_HEADS * D_K, D_MODEL))
        return {'x': x, 'w_q': w_q, 'w_k': w_k, 'w_v': w_v, 'w_o': w_o}
    _L1_attn_in = _L1_attn_setup()

    def _L1_ffn_setup():
        import jax, jax.numpy as jnp
        import numpy as np
        from jax import lax
        DIM = 256
        N_EXPERTS = 16
        TOPK = 4
        N_GROUPS = 4
        TOPK_GROUPS = 2
        ROUTE_SCALE = 1.0
        INTER = 128
        SHARED_INTER = 2 * INTER

        def _gate(x, gate_w):
            T = x.shape[0]
            logits = x @ gate_w.T
            scores = jax.nn.softmax(logits.astype(jnp.float32), axis=-1)
            original_scores = scores
            g = scores.reshape(T, N_GROUPS, N_EXPERTS // N_GROUPS)
            group_scores = g.max(axis=-1)
            _, gidx = lax.top_k(group_scores, TOPK_GROUPS)
            gmask = jnp.zeros_like(group_scores).at[jnp.arange(T)[:, None], gidx].set(1.0)
            masked = (g * gmask[..., None]).reshape(T, N_EXPERTS)
            _, indices = lax.top_k(masked, TOPK)
            weights = jnp.take_along_axis(original_scores, indices, axis=1)
            weights = weights * ROUTE_SCALE
            return (weights.astype(x.dtype), indices)
        key = jax.random.key(seed)
        ks = jax.random.split(key, 8)
        s = lambda fan_in: 1.0 / np.sqrt(fan_in)
        return {'x': jax.random.normal(ks[0], (2, 256, DIM), dtype=jnp.float32), 'gate_w': jax.random.normal(ks[1], (N_EXPERTS, DIM), dtype=jnp.float32) * s(DIM), 'w1': jax.random.normal(ks[2], (N_EXPERTS, DIM, INTER), dtype=jnp.float32) * s(DIM), 'w2': jax.random.normal(ks[3], (N_EXPERTS, INTER, DIM), dtype=jnp.float32) * s(INTER), 'w3': jax.random.normal(ks[4], (N_EXPERTS, DIM, INTER), dtype=jnp.float32) * s(DIM), 'ws1': jax.random.normal(ks[5], (DIM, SHARED_INTER), dtype=jnp.float32) * s(DIM), 'ws2': jax.random.normal(ks[6], (SHARED_INTER, DIM), dtype=jnp.float32) * s(SHARED_INTER), 'ws3': jax.random.normal(ks[7], (DIM, SHARED_INTER), dtype=jnp.float32) * s(DIM)}
    _L1_ffn_in = _L1_ffn_setup()
    _d = {'L0_attn_x': _L0_attn_in['x'], 'L0_attn_wq': _L0_attn_in['wq'], 'L0_attn_wk': _L0_attn_in['wk'], 'L0_attn_wv': _L0_attn_in['wv'], 'L0_attn_in_proj_w': _L0_attn_in['in_proj_w'], 'L0_attn_in_proj_b': _L0_attn_in['in_proj_b'], 'L0_attn_out_w': _L0_attn_in['out_w'], 'L0_attn_out_b': _L0_attn_in['out_b'], 'L0_ffn_Wg': _L0_ffn_in['Wg'], 'L0_ffn_W1': _L0_ffn_in['W1'], 'L0_ffn_b1': _L0_ffn_in['b1'], 'L0_ffn_W2': _L0_ffn_in['W2'], 'L0_ffn_b2': _L0_ffn_in['b2'], 'L1_attn_w_q': _L1_attn_in['w_q'], 'L1_attn_w_k': _L1_attn_in['w_k'], 'L1_attn_w_v': _L1_attn_in['w_v'], 'L1_attn_w_o': _L1_attn_in['w_o'], 'L1_ffn_gate_w': _L1_ffn_in['gate_w'], 'L1_ffn_w1': _L1_ffn_in['w1'], 'L1_ffn_w2': _L1_ffn_in['w2'], 'L1_ffn_w3': _L1_ffn_in['w3'], 'L1_ffn_ws1': _L1_ffn_in['ws1'], 'L1_ffn_ws2': _L1_ffn_in['ws2'], 'L1_ffn_ws3': _L1_ffn_in['ws3']}
    _x0 = _d['L0_attn_x']
    _d['L0_attn_x'] = jax.random.normal(jax.random.fold_in(jax.random.key(seed), 1), (8, 512, 256), dtype=_x0.dtype)
    del _x0
    return _d

def reference(L0_attn_x, L0_attn_wq, L0_attn_wk, L0_attn_wv, L0_attn_in_proj_w, L0_attn_in_proj_b, L0_attn_out_w, L0_attn_out_b, L0_ffn_Wg, L0_ffn_W1, L0_ffn_b1, L0_ffn_W2, L0_ffn_b2, L1_attn_w_q, L1_attn_w_k, L1_attn_w_v, L1_attn_w_o, L1_ffn_gate_w, L1_ffn_w1, L1_ffn_w2, L1_ffn_w3, L1_ffn_ws1, L1_ffn_ws2, L1_ffn_ws3):

    def _L0_attn_ref(x, wq, wk, wv, in_proj_w, in_proj_b, out_w, out_b):
        import jax, jax.numpy as jnp
        import numpy as np
        B, M, D, H = (2, 512, 256, 16)

        def _rope(x):
            b, m, d = x.shape
            i = jnp.arange(d // 2, dtype=jnp.float32)
            theta = 10000.0 ** (-2.0 * (i - 1.0) / d)
            ang = jnp.arange(m, dtype=jnp.float32)[:, None] * theta[None, :]
            c, s = (jnp.cos(ang), jnp.sin(ang))
            xe, xo = (x[..., 0::2], x[..., 1::2])
            ye = xe * c + xo * s
            yo = -xe * s + xo * c
            return jnp.stack([ye, yo], axis=-1).reshape(b, m, d)
        b, m, d = x.shape
        h = H
        hd = d // h
        q = _rope(x @ wq.T)
        k = _rope(x @ wk.T)
        v = _rope(x @ wv.T)
        wqi, wki, wvi = jnp.split(in_proj_w, 3, axis=0)
        bqi, bki, bvi = jnp.split(in_proj_b, 3, axis=0)
        qh = (q @ wqi.T + bqi).reshape(b, m, h, hd)
        kh = (k @ wki.T + bki).reshape(b, m, h, hd)
        vh = (v @ wvi.T + bvi).reshape(b, m, h, hd)
        scores = jnp.einsum('bqhd,bkhd->bhqk', qh, kh) / jnp.sqrt(jnp.float32(hd))
        causal = jnp.tril(jnp.ones((m, m), dtype=bool))
        scores = jnp.where(causal, scores, jnp.float32(-jnp.inf))
        attn = jax.nn.softmax(scores, axis=-1)
        o = jnp.einsum('bhqk,bkhd->bqhd', attn, vh).reshape(b, m, d)
        return o @ out_w.T + out_b

    def _L0_ffn_ref(x, Wg, W1, b1, W2, b2):
        import jax, jax.numpy as jnp
        import numpy as np
        B, L, H, E, FF, C = (4, 512, 256, 8, 1024, 2)
        b, l, h = x.shape
        e = Wg.shape[1]
        n = b * l
        k = min(max(int(n * C / e), 1), n)
        xt = x.reshape(n, h)
        S = jax.nn.sigmoid(xt @ Wg).T
        G, I = jax.lax.top_k(S, k)
        ex = xt[I]
        hid = jax.nn.gelu(jnp.einsum('ekh,ehf->ekf', ex, W1) + b1[:, None, :], approximate=False)
        out = (jnp.einsum('ekf,efh->ekh', hid, W2) + b2[:, None, :]) * G[..., None]
        new_x = jnp.zeros_like(xt).at[I.reshape(-1)].add(out.reshape(-1, h))
        return new_x.reshape(b, l, h)

    def _L1_attn_ref(x, w_q, w_k, w_v, w_o):
        import jax, jax.numpy as jnp
        import numpy as np
        D_K, D_MODEL, NUM_HEADS = (64, 256, 16)

        def _xavier(key, shape):
            fan_in, fan_out = (shape[-2], shape[-1])
            limit = float(np.sqrt(6.0 / (fan_in + fan_out)))
            return jax.random.uniform(key, shape, jnp.float32, -limit, limit)
        scale = 1.0 / jnp.sqrt(jnp.asarray(D_K, dtype=jnp.float32))
        q = jnp.einsum('bsd,hdk->bhsk', x, w_q)
        k = jnp.einsum('bsd,hdk->bhsk', x, w_k)
        v = jnp.einsum('bsd,hdk->bhsk', x, w_v)
        scores = jnp.einsum('bhqk,bhmk->bhqm', q, k) * scale
        weights = jax.nn.softmax(scores, axis=-1)
        z = jnp.einsum('bhqm,bhmk->bhqk', weights, v)
        b, h, s, dk = z.shape
        z = jnp.transpose(z, (0, 2, 1, 3)).reshape(b, s, h * dk)
        z = jnp.einsum('bse,ed->bsd', z, w_o)
        return x + z

    def _L1_ffn_ref(x, gate_w, w1, w2, w3, ws1, ws2, ws3):
        import jax, jax.numpy as jnp
        import numpy as np
        from jax import lax
        DIM = 256
        N_EXPERTS = 16
        TOPK = 4
        N_GROUPS = 4
        TOPK_GROUPS = 2
        ROUTE_SCALE = 1.0
        INTER = 128
        SHARED_INTER = 2 * INTER

        def _gate(x, gate_w):
            T = x.shape[0]
            logits = x @ gate_w.T
            scores = jax.nn.softmax(logits.astype(jnp.float32), axis=-1)
            original_scores = scores
            g = scores.reshape(T, N_GROUPS, N_EXPERTS // N_GROUPS)
            group_scores = g.max(axis=-1)
            _, gidx = lax.top_k(group_scores, TOPK_GROUPS)
            gmask = jnp.zeros_like(group_scores).at[jnp.arange(T)[:, None], gidx].set(1.0)
            masked = (g * gmask[..., None]).reshape(T, N_EXPERTS)
            _, indices = lax.top_k(masked, TOPK)
            weights = jnp.take_along_axis(original_scores, indices, axis=1)
            weights = weights * ROUTE_SCALE
            return (weights.astype(x.dtype), indices)
        shape = x.shape
        xt = x.reshape(-1, DIM)
        T = xt.shape[0]
        weights, indices = _gate(xt, gate_w)
        c = jnp.zeros((T, N_EXPERTS), dtype=xt.dtype)
        c = c.at[jnp.arange(T)[:, None], indices].add(weights)
        h1 = jnp.einsum('td,edi->tei', xt, w1)
        h3 = jnp.einsum('td,edi->tei', xt, w3)
        a = jax.nn.silu(h1) * h3
        y = jnp.einsum('tei,eid,te->td', a, w2, c)
        z = jax.nn.silu(xt @ ws1) * (xt @ ws3) @ ws2
        return (y + z).reshape(shape)
    x = L0_attn_x
    x = x + 0.5 * _L0_ffn_ref(_layernorm(x, axis=-1), L0_ffn_Wg, L0_ffn_W1, L0_ffn_b1, L0_ffn_W2, L0_ffn_b2)
    x = x + _L0_attn_ref(_layernorm(x, axis=-1), L0_attn_wq, L0_attn_wk, L0_attn_wv, L0_attn_in_proj_w, L0_attn_in_proj_b, L0_attn_out_w, L0_attn_out_b)
    x = x + 0.5 * _L0_ffn_ref(_layernorm(x, axis=-1), L0_ffn_Wg, L0_ffn_W1, L0_ffn_b1, L0_ffn_W2, L0_ffn_b2)
    x = x + 0.5 * _L1_ffn_ref(_layernorm(x, axis=-1), L1_ffn_gate_w, L1_ffn_w1, L1_ffn_w2, L1_ffn_w3, L1_ffn_ws1, L1_ffn_ws2, L1_ffn_ws3)
    x = x + _L1_attn_ref(_layernorm(x, axis=-1), L1_attn_w_q, L1_attn_w_k, L1_attn_w_v, L1_attn_w_o)
    x = x + 0.5 * _L1_ffn_ref(_layernorm(x, axis=-1), L1_ffn_gate_w, L1_ffn_w1, L1_ffn_w2, L1_ffn_w3, L1_ffn_ws1, L1_ffn_ws2, L1_ffn_ws3)
    return x

_drawn_inputs = setup_inputs


def setup_inputs(seed=0):
    import zlib

    import numpy as np

    out = dict(_drawn_inputs(seed))
    spreads = {'L0_ffn_b1': (0.0, 0.1), 'L0_ffn_b2': (0.0, 0.1)}
    factors = {'L0_attn_wq': 8.0,
     'L0_attn_wk': 8.0,
     'L0_attn_wv': 8.0,
     'L0_attn_in_proj_w': 8.0,
     'L0_attn_in_proj_b': 5.688,
     'L0_attn_out_w': 4.64,
     'L0_attn_out_b': 8.0,
     'L1_ffn_gate_w': 3.149,
     'L1_ffn_w1': 3.005,
     'L1_ffn_w2': 2.827,
     'L1_ffn_w3': 2.815}
    for name, (base, spread) in spreads.items():
        noise = np.random.default_rng([zlib.crc32(name.encode()), seed]).standard_normal(out[name].shape)
        drawn = base * np.exp(spread * noise) if base else spread * noise
        out[name] = jnp.asarray(drawn.astype(out[name].dtype))
    for name, factor in factors.items():
        out[name] = (out[name] * factor).astype(out[name].dtype)
    return out
```

```python
import concourse.bass as bass
from concourse import mybir
from contextlib import ExitStack
import numpy as np

F32 = mybir.dt.float32
F32R = mybir.dt.float32r
BF16 = mybir.dt.bfloat16
I32 = mybir.dt.int32
ALU = mybir.AluOpType
ACT = mybir.ActivationFunctionType
AX = mybir.AxisListType
ds = bass.ds

P = 128
TOK, D = 4096, 256
NT = TOK // P
KC = D // P
GT = 4
GTOK = GT * P
NG = NT // GT
BATCH, SEQ = 8, 512
EPS = 1e-5

E0, CAP, FF = 8, 1024, 1024
FC = FF // P
CC = CAP // P
SEG = P // E0
NSTEP = 28
ROW = D + E0

C_ID, C_BLK, C_TRI, C_POW, C_IOTA, C_PART, C_TILE, C_END = 0, 128, 256, 384, 416, 544, 545, 577


class Steps:

    def __init__(self, eng, sem):
        self.eng, self.sem, self.base, self.n = eng, sem, 0, 0

    def mark(self, ins):
        ins.then_inc(self.sem, 1)
        self.n += 1

    def link(self, ins):
        self.mark(ins)
        self.wait()

    def wait(self):
        self.eng.wait_ge(self.sem, self.base + self.n)

    def enter(self, base):
        self.base, self.n = base, 0


def mm3(pe, out, a_hi, a_lo, b_hi, b_lo, start, stop):
    pe.matmul(out, a_hi, b_hi, start=start, stop=False, skip_group_check=True)
    pe.matmul(out, a_hi, b_lo, start=False, stop=False, skip_group_check=True)
    return pe.matmul(out, a_lo, b_hi, start=False, stop=stop, skip_group_check=True)


def row_stats(dve, st, arrived, xs, stats, mean, var, rstd, tmp, half):
    for t in range(stats.shape[1]):
        if t % GT == 0:
            arrived(t // GT)
        last = dve.bn_stats(stats[:, t], xs[:, t])
    st.link(last)
    me, mo = stats[:, :, 1], stats[:, :, 4]
    st.mark(dve.tensor_tensor(mean[:], me, mo, ALU.add))
    st.mark(dve.tensor_tensor(tmp[:], me, mo, ALU.subtract))
    st.link(dve.tensor_tensor(var[:], stats[:, :, 2], stats[:, :, 5], ALU.add))
    st.link(dve.tensor_tensor(tmp[:], tmp[:], tmp[:], ALU.mult))
    st.mark(dve.tensor_scalar(mean[:], mean[:], 0.5, None, ALU.mult))
    st.mark(dve.tensor_scalar(tmp[:], tmp[:], 0.25, EPS, ALU.mult, ALU.add))
    st.wait()
    st.link(dve.scalar_tensor_tensor(var[:], var[:], 1.0 / D, tmp[:], ALU.mult, ALU.add))
    st.link(dve.tensor_scalar(half[:], var[:].bitcast(I32), 1, None, ALU.logical_shift_right))
    st.link(dve.tensor_scalar(rstd[:].bitcast(I32), half[:], -1.0, float(0x5F3759DF), ALU.mult, ALU.add))
    for _ in range(4):
        st.link(dve.tensor_tensor(tmp[:], rstd[:], rstd[:], ALU.mult))
        st.link(dve.tensor_tensor(tmp[:], tmp[:], var[:], ALU.mult))
        st.link(dve.tensor_scalar(tmp[:], tmp[:], -0.5, 1.5, ALU.mult, ALU.add))
        st.link(dve.tensor_tensor(rstd[:], rstd[:], tmp[:], ALU.mult))


class Pools:
    SMALL, PACK = 256, 1024

    def __init__(self, nc, ctx, tag):
        self.nc, self.ctx, self.tag = nc, ctx, tag
        self.packs, self.at = 0, self.PACK
        ctx.enter_context(nc.cleanup_on_exit())

    def sb(self, name, shape, dt=F32):
        words = int(np.prod(shape[1:]))
        if words > self.SMALL or dt not in (F32, I32) or shape[0] != P:
            return self.ctx.enter_context(self.nc.sbuf_tensor(f"{self.tag}_{name}", shape, dt))
        if self.at + words > self.PACK:
            self.pack = self.ctx.enter_context(self.nc.sbuf_tensor(f"{self.tag}_small{self.packs}", [P, self.PACK], F32))
            self.packs, self.at = self.packs + 1, 0
        part = self.pack[:, self.at:self.at + words]
        self.at += words
        if dt != F32:
            part = part.bitcast(dt)
        dims = "abcd"[:len(shape) - 1]
        if len(dims) > 1:
            part = part.rearrange(f"p ({' '.join(dims)}) -> p {' '.join(dims)}", **dict(zip(dims, shape[1:])))
        return part

    def ps(self, name, shape, dt=F32):
        return self.ctx.enter_context(self.nc.psum_tensor(f"{self.tag}_{name}", shape, dt))

    def sem(self, name):
        return self.nc.alloc_semaphore(name=f"{self.tag}_{name}")


def ffn0_route(nc, tag, x_in, x_out, rows, wg, const, idx):
    with ExitStack() as ctx:
        pool = Pools(nc, ctx, tag)
        sb, ps, sem = pool.sb, pool.ps, pool.sem
        xs = sb("xs", [P, NT, D])
        xn = sb("xn", [P, 2, GT, D])
        xT = sb("xT", [P, 2, KC, GTOK])
        stats = sb("stats", [P, NT, 6])
        mean, var, rstd, tmp = (sb(n, [P, NT]) for n in ("mean", "var", "rstd", "tmp"))
        half = sb("half", [P, NT], I32)
        wg_sb = sb("wg", [P, KC, E0])
        logit = sb("logit", [P, E0, NT])
        gate = sb("gate", [P, NT, E0])
        lk = sb("lk", [P, 2 * P])
        top = sb("top", [P, 4])
        bound = sb("bound", [P, 1])
        steps = sb("steps", [P, NSTEP + 1])
        lo, cand, count, got, high = (sb(n, [P, 1]) for n in ("lo", "cand", "count", "got", "high"))
        over, tie, ge, pre_over, pre_tie = (sb(n, [P, 2 * P]) for n in ("over", "tie", "ge", "pre_over", "pre_tie"))
        tot2 = sb("tot2", [P, 2])
        offs = sb("offs", [P, 4])
        off_tie = sb("off_tie", [P, 1])
        place = sb("place", [P, 2 * P])
        slot_i, col_i, row_i = (sb(n, [P, 2, E0, SEG], I32) for n in ("slot_i", "col_i", "row_i"))
        col_f, row_f = (sb(n, [P, 2, E0, SEG]) for n in ("col_f", "row_f"))
        iota8 = sb("iota8", [P, CC])
        iota_b = sb("iota_b", [P, P], BF16)
        hot_c = sb("hot_c", [P, 2 * E0 * SEG, CC])
        ids = sb("ids", [P, 2 * E0 * SEG, 2 * CC], BF16)
        NA = 8
        hot_r = sb("hot_r", [P, NA, P], BF16)
        id_sb = sb("id_sb", [P, E0, 2 * CC])
        tp = ps("tp", [P, 2, 2, 512])
        lg = ps("lg", [P, NT, E0])
        lt = ps("lt", [P, 512])
        sm = ps("sm", [P, 512])
        idp = ps("idp", [P, E0, 2 * CC])

        loaded, c_loaded = [sem(f"loaded{g}") for g in range(NG)], sem("c_loaded")
        xn_ready, xn_stored = sem("xn_ready"), [sem("xn_stored0"), sem("xn_stored1")]
        tp_ready, xt_ready, lg_ready = sem("tp_ready"), sem("xt_ready"), sem("lg_ready")
        gate_ready, own, stored, act_own = sem("gate_ready"), sem("own"), sem("stored"), sem("act_own")
        pe_done, dve_for_pe = sem("pe_done"), sem("dve_for_pe")
        cnt_ready, tot_ready = sem("cnt_ready"), sem("tot_ready")
        hot_ready, hot_used, idp_ready = sem("hot_ready"), sem("hot_used"), sem("idp_ready")

        xv = x_in.rearrange("(t p) d -> p t d", p=P)
        ov = x_out.rearrange("(t p) d -> p t d", p=P)
        rv = rows.rearrange("(t p) d -> p t d", p=P)
        ident = const[:, C_ID:C_ID + P]
        same_expert = const[:, C_BLK:C_BLK + P]
        before = const[:, C_TRI:C_TRI + P]
        block = ctx.enter_context(nc.Block())

        @block.sync
        def _(sp):
            for g in range(NG):
                sp.dma_start(xs[:, g * GT:(g + 1) * GT], xv[:, g * GT:(g + 1) * GT]).then_inc(loaded[g], 16)
                if g == 0:
                    sp.dma_start(wg_sb[:], wg.rearrange("(k p) e -> p k e", p=P)).then_inc(c_loaded, 16)
            for g in range(NG):
                sp.wait_ge(loaded[g], 16)
                sp.dma_start(ov[:, g * GT:(g + 1) * GT], xs[:, g * GT:(g + 1) * GT]).then_inc(stored, 16)
            sp.wait_ge(gate_ready, 1)
            sp.dma_start(rv[:, :, D:ROW], gate[:]).then_inc(stored, 16)
            sp.wait_ge(stored, 16 * (NG + 1))

        @block.gpsimd
        def _(pool_e):
            for g in range(NG):
                pool_e.wait_ge(xn_ready, g + 1)
                pool_e.dma_start(rv[:, g * GT:(g + 1) * GT, 0:D], xn[:, g % 2]).then_inc(xn_stored[g % 2], 16)
            pool_e.wait_ge(xn_stored[0], 16 * NG // 2)
            pool_e.wait_ge(xn_stored[1], 16 * NG // 2)

        @block.scalar
        def _(act):
            for g in range(NG):
                act.wait_ge(tp_ready, g + 1)
                if g >= 2:
                    act.wait_ge(lg_ready, g - 1)
                for k in range(KC):
                    last = act.activation(xT[:, g % 2, k], tp[:, g % 2, k], ACT.Copy)
                last.then_inc(xt_ready, 1)
            act.wait_ge(dve_for_pe, 1)
            act.activation(gate[:], logit[:].rearrange("p e t -> p t e"), ACT.Sigmoid).then_inc(act_own, 1)
            act.wait_ge(act_own, 1)
            act.activation(gate[:], gate[:], ACT.Copy, scale=0.5).then_inc(gate_ready, 1)

        @block.tensor
        def _(pe):
            def transposes(g):
                pe.wait_ge(xn_ready, g + 1)
                if g >= 2:
                    pe.wait_ge(xt_ready, g - 1)
                for t in range(GT):
                    for k in range(KC):
                        last = pe.transpose(tp[:, g % 2, k, t * P:(t + 1) * P], xn[:, g % 2, t, k * P:(k + 1) * P], ident)
                last.then_inc(tp_ready, 1)

            def logits(g):
                pe.wait_ge(xt_ready, g + 1)
                for t in range(GT):
                    for k in range(KC):
                        last = pe.matmul(lg[:, g * GT + t], xT[:, g % 2, k, t * P:(t + 1) * P], wg_sb[:, k],
                                         start=(k == 0), stop=(k == KC - 1), skip_group_check=True)
                last.then_inc(lg_ready, 1)

            pe.wait_ge(c_loaded, 16)
            transposes(0)
            for g in range(NG):
                if g + 1 < NG:
                    transposes(g + 1)
                logits(g)
            pe.wait_ge(dve_for_pe, 1)
            for h in range(2):
                last = pe.transpose(lt[:, h * P:(h + 1) * P], logit[:].rearrange("p e (s h) -> p h (e s)", h=2)[:, h], ident)
            last.then_inc(pe_done, 1)
            pe.wait_ge(dve_for_pe, 2)
            pe.transpose(sm[0:1, 0:P], top[:, 0:1], ident).then_inc(pe_done, 1)
            pe.wait_ge(dve_for_pe, 3)
            pe.matmul(sm[:, 128:129], const[0:1, C_POW:C_POW + 1].to_broadcast([1, P]),
                      top[0:1, 1:2], start=True, stop=True).then_inc(pe_done, 1)
            with pe.Fori(0, NSTEP) as i:
                pe.wait_ge(cnt_ready, i + 1)
                pe.matmul(sm[:, 0:1], same_expert, count[:], start=True, stop=True).then_inc(tot_ready, 1)
            pe.wait_ge(dve_for_pe, 4)
            pe.matmul(sm[:, 0:2], before, tot2[:], start=True, stop=True)
            pe.matmul(sm[:, 2:4], same_expert, tot2[:], start=True, stop=True, skip_group_check=True).then_inc(pe_done, 1)
            pe.wait_ge(dve_for_pe, 5)
            for h in range(2):
                last = pe.transpose(lt[:, h * P:(h + 1) * P], place[:, h * P:(h + 1) * P], ident)
            last.then_inc(pe_done, 1)
            pe.wait_ge(dve_for_pe, 6)
            for e in range(E0):
                for t in range(NT):
                    n = e * NT + t
                    pe.wait_ge(hot_ready, n + 1)
                    col = (t % 2) * E0 * SEG + e * SEG + t // 2
                    last = pe.matmul(idp[:, e], hot_r[:, n % NA], ids[:, col], start=(t == 0), stop=(t == NT - 1),
                                     skip_group_check=True)
                    last.then_inc(hot_used, 1)

        @block.vector
        def _(dve):
            st = Steps(dve, own)
            row_stats(dve, st, lambda g: dve.wait_ge(loaded[g], 16), xs, stats, mean, var, rstd, tmp, half)
            for g in range(NG):
                if g >= 2:
                    dve.wait_ge(xn_stored[g % 2], 16 * (g // 2))
                    dve.wait_ge(tp_ready, g - 1)
                for t in range(GT):
                    n = g * GT + t
                    last = dve.tensor_scalar(xn[:, g % 2, t], xs[:, n], mean[:, n:n + 1], rstd[:, n:n + 1],
                                             ALU.subtract, ALU.mult)
                last.then_inc(xn_ready, 1)
            dve.wait_ge(lg_ready, NG)
            dve.tensor_copy(logit[:], lg[:].rearrange("p t e -> p e t")).then_inc(dve_for_pe, 1)
            dve.wait_ge(pe_done, 1)
            st.link(dve.tensor_copy(lk[:], lt[:, 0:2 * P]))
            dve.tensor_reduce(top[:, 0:1], lk[:], AX.X, ALU.max, apply_absolute_value=True).then_inc(dve_for_pe, 1)
            dve.wait_ge(pe_done, 2)
            st.link(dve.tensor_reduce(top[0:1, 2:3], sm[0:1, 0:P], AX.X, ALU.max))
            dve.tensor_scalar(top[0:1, 1:2], top[0:1, 2:3], 1.001, 1e-30, ALU.mult, ALU.add).then_inc(dve_for_pe, 1)
            dve.wait_ge(pe_done, 3)
            st.link(dve.tensor_copy(bound[:], sm[:, 128:129]))
            st.mark(dve.tensor_scalar(steps[:], const[:, C_POW:C_POW + NSTEP + 1], bound[:], None, ALU.mult))
            st.mark(dve.tensor_scalar(lo[:], bound[:], -1.0, None, ALU.mult))
            st.link(dve.tensor_scalar(cand[:], bound[:], 0.0, None, ALU.mult))
            base = st.n
            with dve.Fori(0, NSTEP) as i:
                st.enter(i * 3 + base)
                dve.tensor_scalar(ge[:], lk[:], cand[:], None, ALU.is_ge, ALU.add, accum_out=count[:]).then_inc(cnt_ready, 1)
                dve.wait_ge(tot_ready, i + 1)
                st.link(dve.tensor_scalar(got[:], sm[:, 0:1], CAP - 0.5, steps[:, ds(i, 1)], ALU.is_ge, ALU.mult))
                st.mark(dve.tensor_scalar(cand[:], lo[:], got[:], steps[:, ds(i + 1, 1)], ALU.add, ALU.add))
                st.mark(dve.tensor_scalar(lo[:], lo[:], got[:], None, ALU.add))
                st.wait()
            st.enter(NSTEP * 3 + base)
            st.link(dve.tensor_scalar(high[:], lo[:], steps[:, NSTEP - 1:NSTEP], None, ALU.add))
            st.mark(dve.tensor_scalar(over[:], lk[:], high[:], None, ALU.is_ge))
            st.mark(dve.tensor_scalar(ge[:], lk[:], lo[:], None, ALU.is_ge))
            st.wait()
            st.link(dve.tensor_tensor(tie[:], ge[:], over[:], ALU.subtract))
            st.mark(dve.tensor_tensor_scan(pre_over[:], over[:], over[:], 0.0, ALU.add, ALU.bypass))
            st.link(dve.tensor_tensor_scan(pre_tie[:], tie[:], tie[:], 0.0, ALU.add, ALU.bypass))
            dve.tensor_copy(tot2[:, 0:1], pre_over[:, 2 * P - 1:2 * P])
            dve.tensor_copy(tot2[:, 1:2], pre_tie[:, 2 * P - 1:2 * P]).then_inc(dve_for_pe, 1)
            dve.wait_ge(pe_done, 4)
            st.link(dve.tensor_copy(offs[:], sm[:, 0:4]))
            st.link(dve.tensor_tensor(off_tie[:], offs[:, 1:2], offs[:, 2:3], ALU.add))
            st.mark(dve.scalar_tensor_tensor(pre_over[:], pre_over[:], offs[:, 0:1], over[:], ALU.add, ALU.mult))
            st.link(dve.scalar_tensor_tensor(pre_tie[:], pre_tie[:], off_tie[:], tie[:], ALU.add, ALU.mult))
            dve.tensor_tensor(place[:], pre_over[:], pre_tie[:], ALU.add).then_inc(dve_for_pe, 1)
            dve.wait_ge(pe_done, 5)
            flat = lambda a: a[:].rearrange("p h e s -> p (h e s)")
            st.link(dve.tensor_scalar(flat(slot_i), lt[:, 0:2 * P], -1.0, None, ALU.add))
            st.mark(dve.tensor_scalar(flat(col_i), flat(slot_i), 7, None, ALU.arith_shift_right))
            st.link(dve.tensor_scalar(flat(row_i), flat(slot_i), 127, None, ALU.bitwise_and))
            st.mark(dve.tensor_copy(flat(col_f), flat(col_i)))
            st.mark(dve.tensor_copy(flat(row_f), flat(row_i)))
            st.mark(dve.tensor_copy(iota8[:], const[:, C_IOTA:C_IOTA + CC]))
            st.link(dve.tensor_copy(iota_b[:], const[:, C_IOTA:C_IOTA + P]))
            n_col = 2 * E0 * SEG
            st.link(dve.tensor_tensor(hot_c[:], flat(col_f).unsqueeze(2).to_broadcast([P, n_col, CC]),
                                      iota8[:].unsqueeze(1).to_broadcast([P, n_col, CC]), ALU.is_equal))
            st.mark(dve.tensor_scalar(ids[:, :, 0:CC], hot_c[:], const[:, C_PART:C_PART + 1], None, ALU.mult))
            for h in range(2):
                tiles = const[:, C_TILE:C_TILE + NT].rearrange("p (s h) -> p h s", h=2)[:, h]
                hv = lambda a: a.rearrange("p (h e s) c -> p h e s c", h=2, e=E0)[:, h]
                for e in range(E0):
                    last = dve.tensor_tensor(hv(ids[:, :, CC:2 * CC])[:, e], hv(hot_c[:])[:, e],
                                      tiles.unsqueeze(2).to_broadcast([P, SEG, CC]), ALU.mult)
            last.then_inc(dve_for_pe, 1)
            for e in range(E0):
                for t in range(NT):
                    n = e * NT + t
                    if n >= NA:
                        dve.wait_ge(hot_used, n - NA + 1)
                    dve.tensor_scalar(hot_r[:, n % NA], iota_b[:], row_f[:, t % 2, e, t // 2:t // 2 + 1], None,
                                      ALU.is_equal).then_inc(hot_ready, 1)
            dve.wait_ge(hot_used, E0 * NT)
            st.link(dve.tensor_copy(id_sb[:], idp[:]))
            dve.scalar_tensor_tensor(idx[:], id_sb[:, :, CC:2 * CC], float(P), id_sb[:, :, 0:CC],
                                     ALU.mult, ALU.add)


def ffn0_experts(nc, tag, rows, x_out, w1, b1, w2, b2, const, idx):
    with ExitStack() as ctx:
        pool = Pools(nc, ctx, tag)
        sb, ps, sem = pool.sb, pool.ps, pool.sem
        HALF = CAP // GTOK
        N = HALF * FC
        WCOL = KC * FF + FC * D
        WP = WCOL // N
        raw = sb("raw", [P, 2, WCOL])
        w_hi, w_lo = sb("w_hi", [P, 2, WCOL], F32R), sb("w_lo", [P, 2, WCOL], F32R)
        b1_sb = sb("b1", [P, 2, FC])
        b2_sb = sb("b2", [P, 2, D])
        xg = sb("xg", [P, CC, ROW])
        gates = sb("gates", [P, 2, CC])
        x_hi, x_lo = sb("x_hi", [P, KC, CAP], F32R), sb("x_lo", [P, KC, CAP], F32R)
        hid = sb("hid", [P, 2, GTOK])
        h_hi, h_lo = sb("h_hi", [P, 2, GTOK], F32R), sb("h_lo", [P, 2, GTOK], F32R)
        y = sb("y", [P, HALF, GT, D])
        h_ps = ps("h_ps", [P, 2, 512])
        t_ps = ps("t_ps", [P, 2, 512])
        o_ps = ps("o_ps", [P, HALF, GT, D])

        b1_in = [sem("b1_in0"), sem("b1_in1")]
        w_in = [sem("w_in0"), sem("w_in1")]
        w_hi_done, w_lo_done = sem("w_hi_done"), sem("w_lo_done")
        b2_in = [sem("b2_in0"), sem("b2_in1")]
        gathered, gates_done = sem("gathered"), sem("gates_done")
        t_ready, x_hi_done, x_lo_done = sem("t_ready"), sem("x_hi_done"), sem("x_lo_done")
        h_ready, hid_ready, hid_hi, hid_lo = sem("h_ready"), sem("hid_ready"), sem("hid_hi"), sem("hid_lo")
        w2_done, y_sum, y_ready, added = (sem(n) for n in ("w2_done", "y_sum", "y_ready", "added"))

        w1v = w1.rearrange("e (k p) f -> e p k f", p=P)
        w2v = w2.rearrange("e (f p) d -> e p f d", p=P)
        b2v = b2.rearrange("e (o d) -> e o d", o=1)
        ident = const[:, C_ID:C_ID + P]
        block = ctx.enter_context(nc.Block())

        def w1_of(part, b, k, f):
            return part[:, b, k * FF + f * P:k * FF + (f + 1) * P]

        def w2_of(part, b, f):
            return part[:, b, KC * FF + f * D:KC * FF + (f + 1) * D]

        def loads_of(e, b):
            return e * 8 + (8 if b else 16)

        @block.sync
        def _(sp):
            def weights(e, b):
                sp.dma_start(raw[:, b, 0:KC * FF].rearrange("p (k f) -> p k f", k=KC), w1v[e]).then_inc(w_in[b], 16)
                sp.dma_start(raw[:, b, KC * FF:WCOL].rearrange("p (f d) -> p f d", f=FC), w2v[e]).then_inc(w_in[b], 16)
                sp.dma_start(b1_sb[:, b], b1[e]).then_inc(b1_in[b], 16)
                sp.dma_start(b2_sb[:, b], b2v[e].to_broadcast([P, D])).then_inc(b2_in[b], 16)

            def following(e, b):
                sp.wait_ge(w_lo_done, (e - 1) * N)
                sp.wait_ge(y_sum, (e - 1) * HALF)
                weights(e, b)

            weights(0, 0)
            weights(1, 1)
            for e in range(2, E0):
                following(e, e % 2)

        @block.gpsimd
        def _(gp):
            def gather(e):
                for c in range(CC):
                    gp.indirect_dma_start(out=xg[:, c], out_offset=None, in_=rows,
                                          in_offset=bass.IndirectOffsetOnAxis(ap=idx[:, e, c:c + 1], axis=0)).then_inc(gathered, 16)

            def body(e, more):
                if more:
                    gp.wait_ge(t_ready, e * (CC // 2) + CC // 2)
                    gp.wait_ge(gates_done, e + 1)
                    gather(e + 1)
                for c in range(CC):
                    if c % GT == 0:
                        gp.wait_ge(y_ready, e * HALF + c // GT + 1)
                    if c == 0 and e > 0:
                        gp.wait_ge(added, e * 16 * CC)
                    gp.indirect_dma_start(out=x_out, out_offset=bass.IndirectOffsetOnAxis(ap=idx[:, e, c:c + 1], axis=0),
                                          in_=y[:, c // GT, c % GT], in_offset=None, compute_op=ALU.add).then_inc(added, 16)
            gather(0)
            for e in range(E0):
                body(e, e + 1 < E0)
            gp.wait_ge(added, E0 * 16 * CC)

        @block.tensor
        def _(pe):
            def transposes(e):
                pe.wait_ge(gathered, (e + 1) * (16 * CC))
                for j in range(CC // 2):
                    if j >= 2:
                        pe.wait_ge(x_lo_done, e * (CC // 2) + (j - 1))
                    for c in range(2):
                        for k in range(KC):
                            last = pe.transpose(t_ps[:, j % 2, (k * 2 + c) * P:(k * 2 + c + 1) * P],
                                                xg[:, 2 * j + c, k * P:(k + 1) * P], ident)
                    last.then_inc(t_ready, 1)

            def up(e, b, n):
                g, f = divmod(n, FC)
                if n == 0:
                    pe.wait_ge(x_lo_done, e * (CC // 2) + CC // 2)
                    pe.wait_ge(w_lo_done, e * N + N)
                if n >= 2 or not isinstance(e, int) or e > 0:
                    pe.wait_ge(hid_ready, e * N + (n - 1))
                for k in range(KC):
                    cols = slice(g * GTOK, (g + 1) * GTOK)
                    last = mm3(pe, h_ps[:, n % 2], w1_of(w_hi, b, k, f), w1_of(w_lo, b, k, f),
                               x_hi[:, k, cols], x_lo[:, k, cols], k == 0, k == KC - 1)
                last.then_inc(h_ready, 1)

            def down(e, b, n):
                g, f = divmod(n, FC)
                pe.wait_ge(hid_lo, e * N + (n + 1))
                if f == 0 and (not isinstance(e, int) or e > 0):
                    pe.wait_ge(y_sum, (e - 1) * HALF + (g + 1))
                for t in range(GT):
                    cols = slice(t * P, (t + 1) * P)
                    last = mm3(pe, o_ps[:, g, t], h_hi[:, n % 2, cols], h_lo[:, n % 2, cols],
                               w2_of(w_hi, b, f), w2_of(w_lo, b, f), f == 0 and t % 2 == 0, f == FC - 1)
                last.then_inc(w2_done, 1)

            def body(e, b, more):
                for n in range(N):
                    up(e, b, n)
                    if n >= 1:
                        down(e, b, n - 1)
                if more:
                    transposes(e + 1)
                down(e, b, N - 1)

            transposes(0)
            body(0, 0, True)
            with pe.Fori(0, E0 // 2 - 1) as i:
                body(i * 2 + 1, 1, True)
                body(i * 2 + 2, 0, True)
            body(E0 - 1, 1, False)

        @block.scalar
        def _(act):
            def split_w(e, b, n):
                if n == 0:
                    act.wait_ge(w_in[b], 32 * (e // 2 + 1) if isinstance(e, int) else 2 * loads_of(e, b))
                    if not isinstance(e, int) or e > 1:
                        act.wait_ge(w2_done, (e - 1) * N)
                cols = slice(n * WP, (n + 1) * WP)
                act.activation(w_hi[:, b, cols], raw[:, b, cols], ACT.Copy).then_inc(w_hi_done, 1)

            def split_x(e):
                for j in range(CC // 2):
                    act.wait_ge(t_ready, e * (CC // 2) + (j + 1))
                    act.activation(x_hi[:, :, j * 2 * P:(j + 1) * 2 * P], t_ps[:, j % 2].rearrange("p (k c) -> p k c", k=KC),
                                   ACT.Copy).then_inc(x_hi_done, 1)

            def body(e, b, more):
                act.wait_ge(b1_in[b], (e // 2 + 1) * 16 if isinstance(e, int) else loads_of(e, b))
                for n in range(N):
                    act.wait_ge(h_ready, e * N + (n + 1))
                    if n >= 2 or not isinstance(e, int) or e > 0:
                        act.wait_ge(hid_lo, e * N + (n - 1))
                    f = n % FC
                    act.activation(hid[:, n % 2], h_ps[:, n % 2], ACT.Gelu, bias=b1_sb[:, b, f:f + 1]).then_inc(hid_ready, 1)
                    if more:
                        split_w(e + 1, 1 - b, n)
                    act.wait_ge(hid_ready, e * N + (n + 1))
                    if n >= 2 or not isinstance(e, int) or e > 0:
                        act.wait_ge(w2_done, e * N + (n - 1))
                    act.activation(h_hi[:, n % 2], hid[:, n % 2], ACT.Copy).then_inc(hid_hi, 1)
                    if n == FC + 1:
                        scale_y(e, b, 0)
                if more:
                    split_x(e + 1)
                scale_y(e, b, 1)

            def scale_y(e, b, g):
                act.wait_ge(y_sum, e * HALF + (g + 1))
                if g == 0:
                    act.wait_ge(gates_done, e + 1)
                for t in range(GT):
                    last = act.activation(y[:, g, t], y[:, g, t], ACT.Copy, scale=gates[:, b, g * GT + t:g * GT + t + 1])
                last.then_inc(y_ready, 1)

            for n in range(N):
                split_w(0, 0, n)
            split_x(0)
            body(0, 0, True)
            with act.Fori(0, E0 // 2 - 1) as i:
                body(i * 2 + 1, 1, True)
                body(i * 2 + 2, 0, True)
            body(E0 - 1, 1, False)

        @block.vector
        def _(dve):
            def split_w(e, b, n):
                dve.wait_ge(w_hi_done, e * N + (n + 1))
                cols = slice(n * WP, (n + 1) * WP)
                dve.tensor_tensor(w_lo[:, b, cols], raw[:, b, cols], w_hi[:, b, cols].bitcast(F32), ALU.subtract).then_inc(w_lo_done, 1)

            def split_x(e, b):
                dve.wait_ge(gathered, (e + 1) * (16 * CC))
                dve.tensor_copy(gates[:, b], xg_gate(e, b)).then_inc(gates_done, 1)
                for j in range(CC // 2):
                    dve.wait_ge(x_hi_done, e * (CC // 2) + (j + 1))
                    cols = slice(j * 2 * P, (j + 1) * 2 * P)
                    dve.tensor_tensor(x_lo[:, :, cols], t_ps[:, j % 2].rearrange("p (k c) -> p k c", k=KC),
                                      x_hi[:, :, cols].bitcast(F32), ALU.subtract).then_inc(x_lo_done, 1)

            def xg_gate(e, b):
                return xg[:, :, D + e] if isinstance(e, int) else xg[:, :, ds(e + D, 1)].rearrange("p c o -> p (c o)")

            def add_b2(e, b, g):
                dve.wait_ge(w2_done, e * N + (g + 1) * FC)
                if g == 0:
                    dve.wait_ge(b2_in[b], (e // 2 + 1) * 16 if isinstance(e, int) else loads_of(e, b))
                if not isinstance(e, int) or e > 0:
                    dve.wait_ge(added, e * (16 * CC))
                dve.tensor_tensor(y[:, g], o_ps[:, g], b2_sb[:, b].unsqueeze(1).to_broadcast([P, GT, D]),
                                  ALU.add).then_inc(y_sum, 1)

            def body(e, b, more):
                for n in range(N):
                    if more:
                        split_w(e + 1, 1 - b, n)
                    dve.wait_ge(hid_hi, e * N + (n + 1))
                    dve.tensor_tensor(h_lo[:, n % 2], hid[:, n % 2], h_hi[:, n % 2].bitcast(F32), ALU.subtract).then_inc(hid_lo, 1)
                    if n == FC:
                        add_b2(e, b, 0)
                if more:
                    split_x(e + 1, 1 - b)
                add_b2(e, b, 1)

            for n in range(N):
                split_w(0, 0, n)
            split_x(0, 0)
            body(0, 0, True)
            with dve.Fori(0, E0 // 2 - 1) as i:
                body(i * 2 + 1, 1, True)
                body(i * 2 + 2, 0, True)
            body(E0 - 1, 1, False)


E1, TOPK, EG, TOPG = 16, 4, 4, 2
UNITS = E1 + 2
INTER = 128
UCOL = 2 * KC * INTER + D


def moe(nc, tag, x_in, x_out, gate_w, w1, w3, w2, const):
    with ExitStack() as ctx:
        pool = Pools(nc, ctx, tag)
        sb, ps, sem = pool.sb, pool.ps, pool.sem
        xs = sb("xs", [P, NT, D])
        x_hi, x_lo = sb("x_hi", [P, KC, TOK], F32R), sb("x_lo", [P, KC, TOK], F32R)
        xn = sb("xn", [P, 2, GT, D])
        stats = sb("stats", [P, NT, 6])
        mean, var, rstd, tmp = (sb(n, [P, NT]) for n in ("mean", "var", "rstd", "tmp"))
        half = sb("half", [P, NT], I32)
        gw, gw_hi, gw_lo = sb("gw", [P, KC, E1]), sb("gw_hi", [P, KC, E1], F32R), sb("gw_lo", [P, KC, E1], F32R)
        coef = sb("coef", [P, NT, UNITS])
        sc = sb("sc", [P, NT, E1])
        q = sb("q", [P, NT, E1])
        q2 = sb("q2", [P, NT, E1])
        best = sb("best", [P, NT, 8])
        r1, r2 = sb("r1", [P, NT]), sb("r2", [P, NT])
        g1, g2 = sb("g1", [P, NT, EG]), sb("g2", [P, NT, EG])
        raw = sb("raw", [P, 2, UCOL])
        w_hi, w_lo = sb("w_hi", [P, 2, UCOL], F32R), sb("w_lo", [P, 2, UCOL], F32R)
        s1, hid = sb("s1", [P, 2, GTOK]), sb("hid", [P, 2, GTOK])
        h_hi, h_lo = sb("h_hi", [P, 2, GTOK], F32R), sb("h_lo", [P, 2, GTOK], F32R)
        h1_ps, h3_ps = ps("h1_ps", [P, 2, 512]), ps("h3_ps", [P, 2, 512])
        o_ps = ps("o_ps", [P, 2, GT, D])

        loaded = [sem(f"loaded{g}") for g in range(NG)]
        c_loaded, own, own_act = sem("c_loaded"), sem("own"), sem("own_act")
        xn_ready, t_ready, x_hi_done, x_lo_done = (sem(n) for n in ("xn_ready", "t_ready", "x_hi_done", "x_lo_done"))
        gw_ready, lg_ready, soft_in, soft_out = (sem(n) for n in ("gw_ready", "lg_ready", "soft_in", "soft_out"))
        w_in, w_hi_done, w_lo_done = [sem("w_in0"), sem("w_in1")], sem("w_hi_done"), sem("w_lo_done")
        h_ready, s1_ready, hid_ready, hid_hi, hid_lo = (sem(n) for n in ("h_ready", "s1_ready", "hid_ready", "hid_hi", "hid_lo"))
        o_ready, o_used, stored = sem("o_ready"), sem("o_used"), sem("stored")

        xv = x_in.rearrange("(t p) d -> p t d", p=P)
        ov = x_out.rearrange("(t p) d -> p t d", p=P)
        ident = const[:, C_ID:C_ID + P]
        block = ctx.enter_context(nc.Block())
        t_ps = [h1_ps, h3_ps]
        lg_ps = o_ps[:].rearrange("p b t d -> p (b t d)")[:, 0:NT * E1].rearrange("p (t e) -> p t e", e=E1)

        def w_of(part, b, which, k):
            c = (which * KC + k) * INTER
            return part[:, b, c:c + INTER]

        def w2_of(part, b):
            return part[:, b, 2 * KC * INTER:UCOL]

        def loads_of(u, b):
            return 48 * (u // 2 + 1) if isinstance(u, int) else u * 24 + (24 if b else 48)

        @block.sync
        def _(sp):
            def weights(u, b):
                for n, w in enumerate((w1, w3)):
                    sp.dma_start(raw[:, b, n * KC * INTER:(n + 1) * KC * INTER].rearrange("p (k i) -> p k i", k=KC),
                                 w[u].rearrange("(k p) i -> p k i", p=P)).then_inc(w_in[b], 16)
                sp.dma_start(raw[:, b, 2 * KC * INTER:UCOL], w2[u]).then_inc(w_in[b], 16)

            sp.dma_start(xs[:, 0:GT], xv[:, 0:GT]).then_inc(loaded[0], 16)
            sp.dma_start(gw[:], gate_w.rearrange("(k p) e -> p k e", p=P)).then_inc(c_loaded, 16)
            weights(0, 0)
            weights(1, 1)
            for g in range(1, NG):
                sp.dma_start(xs[:, g * GT:(g + 1) * GT], xv[:, g * GT:(g + 1) * GT]).then_inc(loaded[g], 16)
            for u in range(2, UNITS):
                sp.wait_ge(w_lo_done, u - 1)
                weights(u, u % 2)
            for g in range(NG):
                sp.wait_ge(o_used, (UNITS - 1) * NG + g + 1)
                sp.dma_start(ov[:, g * GT:(g + 1) * GT], xs[:, g * GT:(g + 1) * GT]).then_inc(stored, 16)
            sp.wait_ge(stored, 16 * NG)

        @block.tensor
        def _(pe):
            def transposes(g):
                pe.wait_ge(xn_ready, g + 1)
                if g >= 2:
                    pe.wait_ge(x_lo_done, g - 1)
                for t in range(GT):
                    for k in range(KC):
                        last = pe.transpose(t_ps[k][:, g % 2, t * P:(t + 1) * P], xn[:, g % 2, t, k * P:(k + 1) * P], ident)
                last.then_inc(t_ready, 1)

            def logits(g):
                pe.wait_ge(x_lo_done, g + 1)
                for t in range(g * GT, (g + 1) * GT):
                    for k in range(KC):
                        last = mm3(pe, lg_ps[:, t], x_hi[:, k, t * P:(t + 1) * P], x_lo[:, k, t * P:(t + 1) * P],
                                   gw_hi[:, k], gw_lo[:, k], k == 0, k == KC - 1)
                last.then_inc(lg_ready, 1)

            pe.wait_ge(c_loaded, 16)
            pe.wait_ge(gw_ready, 2)
            transposes(0)
            for g in range(NG):
                if g + 1 < NG:
                    transposes(g + 1)
                logits(g)

            def up(b, g, first):
                if g == 0:
                    pe.wait_ge(w_lo_done, first // NG + 1)
                if not isinstance(first, int) or first + g >= 2:
                    pe.wait_ge(hid_ready, first + (g - 1))
                for which, out in ((0, h1_ps), (1, h3_ps)):
                    for k in range(KC):
                        cols = slice(g * GTOK, (g + 1) * GTOK)
                        last = mm3(pe, out[:, g % 2], w_of(w_hi, b, which, k), w_of(w_lo, b, which, k),
                                   x_hi[:, k, cols], x_lo[:, k, cols], k == 0, k == KC - 1)
                last.then_inc(h_ready, 1)

            def down(b, g, first):
                n = first + g
                pe.wait_ge(hid_lo, n + 1)
                if isinstance(n, int) and n < 2:
                    pe.wait_ge(soft_in, 2)
                else:
                    pe.wait_ge(o_used, n - 1)
                for t in range(GT):
                    cols = slice(t * P, (t + 1) * P)
                    last = mm3(pe, o_ps[:, g % 2, t], h_hi[:, g % 2, cols], h_lo[:, g % 2, cols],
                               w2_of(w_hi, b), w2_of(w_lo, b), True, True)
                last.then_inc(o_ready, 1)

            def unit(b, first, head):
                for g in range(NG):
                    up(b, g, first)
                    if g >= 1:
                        down(b, g - 1, first)
                    elif not head:
                        down(1 - b, NG - 1, first - NG)

            unit(0, 0, True)
            unit(1, NG, False)
            with pe.Fori(1, UNITS // 2) as i:
                unit(0, i * (2 * NG), False)
                unit(1, i * (2 * NG) + NG, False)
            down(1, NG - 1, (UNITS - 1) * NG)

        @block.scalar
        def _(act):
            st = Steps(act, own_act)
            act.wait_ge(c_loaded, 16)
            act.activation(gw_hi[:], gw[:], ACT.Copy).then_inc(gw_ready, 1)

            def split_w(u, b):
                act.wait_ge(w_in[b], loads_of(u, b))
                if not isinstance(u, int) or u >= 2:
                    act.wait_ge(o_ready, (u - 1) * NG)
                act.activation(w_hi[:, b], raw[:, b], ACT.Copy).then_inc(w_hi_done, 1)

            for g in range(NG):
                act.wait_ge(t_ready, g + 1)
                cols = slice(g * GTOK, (g + 1) * GTOK)
                for k in range(KC):
                    last = act.activation(x_hi[:, k, cols], t_ps[k][:, g % 2], ACT.Copy)
                last.then_inc(x_hi_done, 1)
            split_w(0, 0)
            act.wait_ge(soft_in, 1)
            act.activation(q[:], q[:], ACT.Exp).then_inc(soft_out, 1)

            def step(b, g, first, u):
                n = first + g
                early = isinstance(n, int) and n < 2
                act.wait_ge(h_ready, n + 1)
                if not early:
                    act.wait_ge(hid_ready, n - 1)
                act.activation(s1[:, g % 2], h1_ps[:, g % 2], ACT.Silu).then_inc(s1_ready, 1)
                if g == 2 and u is not None:
                    split_w(u, 1 - b)
                act.wait_ge(hid_ready, n + 1)
                if not early:
                    act.wait_ge(o_ready, n - 1)
                act.activation(h_hi[:, g % 2], hid[:, g % 2], ACT.Copy).then_inc(hid_hi, 1)

            def unit(b, first, u):
                for g in range(NG):
                    step(b, g, first, u)

            unit(0, 0, 1)
            with act.Fori(0, UNITS // 2 - 1) as i:
                unit(1, i * (2 * NG) + NG, i * 2 + 2)
                unit(0, i * (2 * NG) + 2 * NG, i * 2 + 3)
            unit(1, (UNITS - 1) * NG, None)

        @block.vector
        def _(dve):
            st = Steps(dve, own)
            dve.wait_ge(gw_ready, 1)
            dve.tensor_tensor(gw_lo[:], gw[:], gw_hi[:].bitcast(F32), ALU.subtract).then_inc(gw_ready, 1)
            row_stats(dve, st, lambda g: dve.wait_ge(loaded[g], 16), xs, stats, mean, var, rstd, tmp, half)

            def split_w(u, b):
                dve.wait_ge(w_hi_done, u + 1)
                dve.tensor_tensor(w_lo[:, b], raw[:, b], w_hi[:, b].bitcast(F32), ALU.subtract).then_inc(w_lo_done, 1)

            def normalise(g):
                if g >= 2:
                    dve.wait_ge(t_ready, g - 1)
                for t in range(GT):
                    n = g * GT + t
                    last = dve.tensor_scalar(xn[:, g % 2, t], xs[:, n], mean[:, n:n + 1], rstd[:, n:n + 1],
                                             ALU.subtract, ALU.mult)
                last.then_inc(xn_ready, 1)

            normalise(0)
            for g in range(NG):
                if g + 1 < NG:
                    normalise(g + 1)
                dve.wait_ge(x_hi_done, g + 1)
                cols = slice(g * GTOK, (g + 1) * GTOK)
                for k in range(KC):
                    last = dve.tensor_tensor(x_lo[:, k, cols], t_ps[k][:, g % 2], x_hi[:, k, cols].bitcast(F32), ALU.subtract)
                last.then_inc(x_lo_done, 1)
            split_w(0, 0)

            wide = lambda a: a[:].unsqueeze(2).to_broadcast([P, NT, E1])
            dve.wait_ge(lg_ready, NG)
            st.link(dve.tensor_reduce(r1[:], lg_ps, AX.X, ALU.max))
            st.link(dve.tensor_tensor(q[:], lg_ps, wide(r1), ALU.subtract))
            dve.engine_nop().then_inc(soft_in, 2)
            dve.wait_ge(soft_out, 1)
            st.link(dve.tensor_reduce(r1[:], q[:], AX.X, ALU.add))
            st.link(dve.reciprocal(r2[:], r1[:]))
            st.link(dve.tensor_tensor(sc[:], q[:], wide(r2), ALU.mult))
            by_group = lambda a: a[:].rearrange("p t (g m) -> p t g m", g=EG)
            st.link(dve.tensor_reduce(g1[:], by_group(sc), AX.X, ALU.max))
            mine = g1[:].unsqueeze(3).to_broadcast([P, NT, EG, EG])
            other = g1[:].unsqueeze(2).to_broadcast([P, NT, EG, EG])
            st.mark(dve.tensor_tensor(by_group(q), other, mine, ALU.is_gt))
            st.link(dve.tensor_tensor(by_group(q2), other, mine, ALU.is_equal))
            for g in range(EG):
                last = dve.memset(by_group(q2)[:, :, g, g:EG], 0.0)
            st.link(last)
            st.link(dve.tensor_tensor(q[:], q[:], q2[:], ALU.add))
            st.link(dve.tensor_reduce(g2[:], by_group(q), AX.X, ALU.add))
            st.link(dve.tensor_scalar(g1[:], g2[:], TOPG - 0.5, None, ALU.is_lt))
            st.link(dve.tensor_tensor(by_group(q), by_group(sc), g1[:].unsqueeze(3).to_broadcast([P, NT, EG, E1 // EG]), ALU.mult))
            for t in range(NT):
                last = dve.max(best[:, t], q[:, t])
            st.link(last)
            fourth = best[:, :, TOPK - 1:TOPK].to_broadcast([P, NT, E1])
            st.mark(dve.tensor_tensor(q2[:], q[:], fourth, ALU.is_equal))
            st.link(dve.tensor_tensor(q[:], q[:], fourth, ALU.is_gt))
            st.link(dve.tensor_reduce(r1[:], q[:], AX.X, ALU.add))
            flat = lambda a: a[:].rearrange("p t e -> p (t e)")
            keep = coef[:].rearrange("p t u -> p (t u)")[:, 0:NT * E1]
            st.link(dve.memset(keep, 1.0))
            st.link(dve.memset(keep.rearrange("p (t e) -> p t e", e=E1)[:, :, 0], 0.0))
            pre = hid[:, 0, 0:NT * E1]
            st.link(dve.tensor_tensor_scan(pre, keep, flat(q2), 0.0, ALU.mult, ALU.add))
            pre3 = pre.rearrange("p (t e) -> p t e", e=E1)
            st.link(dve.tensor_tensor(pre3, pre3, wide(r1), ALU.add))
            st.link(dve.scalar_tensor_tensor(pre, pre, TOPK + 0.5, flat(q2), ALU.is_lt, ALU.mult))
            st.link(dve.tensor_tensor(q[:], q[:], pre3, ALU.add))
            st.mark(dve.scalar_tensor_tensor(coef[:, :, 0:E1], sc[:], 0.5, q[:], ALU.mult, ALU.mult))
            st.mark(dve.memset(coef[:, :, E1:UNITS], 0.5))
            st.wait()

            def step(b, g, first, u, head=False):
                n = first + g
                early = isinstance(n, int) and n < 2
                dve.wait_ge(s1_ready, n + 1)
                if not early:
                    dve.wait_ge(hid_hi, n - 1)
                dve.tensor_tensor(hid[:, g % 2], s1[:, g % 2], h3_ps[:, g % 2], ALU.mult).then_inc(hid_ready, 1)
                if g == 2 and u is not None:
                    split_w(u, 1 - b)
                dve.wait_ge(hid_hi, n + 1)
                dve.tensor_tensor(h_lo[:, g % 2], hid[:, g % 2], h_hi[:, g % 2].bitcast(F32), ALU.subtract).then_inc(hid_lo, 1)

            def add(g, first, u):
                n = first + g
                dve.wait_ge(o_ready, n + 1)
                if not isinstance(n, int) or n >= NG:
                    dve.wait_ge(o_used, n - (NG - 1))
                for t in range(GT):
                    tile = g * GT + t
                    c = coef[:, tile, u:u + 1] if isinstance(u, int) else coef[:, tile, ds(u, 1)]
                    last = dve.scalar_tensor_tensor(xs[:, tile], o_ps[:, g % 2, t], c, xs[:, tile], ALU.mult, ALU.add)
                last.then_inc(o_used, 1)

            def unit(b, first, u, more):
                for g in range(NG):
                    step(b, g, first, u + 1 if more else None)
                    if g >= 1:
                        add(g - 1, first, u)
                    elif not isinstance(u, int) or u > 0:
                        add(NG - 1, first - NG, u - 1)

            unit(0, 0, 0, True)
            with dve.Fori(0, UNITS // 2 - 1) as i:
                unit(1, i * (2 * NG) + NG, i * 2 + 1, True)
                unit(0, i * (2 * NG) + 2 * NG, i * 2 + 2, True)
            unit(1, (UNITS - 1) * NG, UNITS - 1, False)
            add(NG - 1, (UNITS - 1) * NG, UNITS - 1)


H0, DK0 = 16, 16
OCT = 8
QT = SEQ // P
UNIT = 8
AHEAD = 2
RING = 3


def attention0(nc, tag, x_in, x_out, wq, wk, wv, wqi, wki, wvi, b_in, b_row, wo, rope, mask, const):
    SCALE = DK0 ** -0.5
    with ExitStack() as ctx:
        pool = Pools(nc, ctx, tag)
        sb, ps, sem = pool.sb, pool.ps, pool.sem
        WC = KC * D
        NW = 7
        raw = sb("raw", [P, 2, WC])
        w_hi, w_lo = sb("w_hi", [P, NW, WC], F32R), sb("w_lo", [P, NW, WC], F32R)
        bias = sb("bias", [P, 2, KC])
        rows_b = sb("rows_b", [P, 2, D])
        cos, sin = sb("cos", [P, SEQ]), sb("sin", [P, SEQ])
        even_odd = sb("even_odd", [P, 2])
        mask_f, ident_b, mask_b = sb("mask_f", [P, P]), sb("ident_b", [P, P], BF16), sb("mask_b", [P, P], BF16)
        xs, xn, x_res, y = (sb(n, [P, GT, D]) for n in ("xs", "xn", "x_res", "y"))
        stats = sb("stats", [P, GT, 6])
        mean, var, rstd, tmp = (sb(n, [P, GT]) for n in ("mean", "var", "rstd", "tmp"))
        half = sb("half", [P, GT], I32)
        x_hi, x_lo = sb("x_hi", [P, KC, SEQ], F32R), sb("x_lo", [P, KC, SEQ], F32R)
        turn = sb("turn", [P, 4, SEQ])
        r_f, r_hi, r_lo = sb("r_f", [P, KC, SEQ]), sb("r_hi", [P, KC, SEQ], F32R), sb("r_lo", [P, KC, SEQ], F32R)
        q_hi, q_lo = sb("q_hi", [P, 2, KC, SEQ], F32R), sb("q_lo", [P, 2, KC, SEQ], F32R)
        kf_hi, kf_lo = sb("kf_hi", [P, KC, SEQ], F32R), sb("kf_lo", [P, KC, SEQ], F32R)
        k_hi, k_lo = sb("k_hi", [P, 2, 2, KC, SEQ], F32R), sb("k_lo", [P, 2, 2, KC, SEQ], F32R)
        v = sb("v", [P, 2, QT, H0 // 2, 2, 2 * DK0])
        mx, nmx = sb("mx", [P, RING]), sb("nmx", [P, RING])
        sums, inv = sb("sums", [P, 2, UNIT]), sb("inv", [P, 2, UNIT])
        prob = sb("prob", [P, RING, SEQ])
        pt = sb("pt", [P, 2, UNIT, QT, P])
        wide = sb("wide", [P, 2, P])
        rt, zf = sb("rt", [P, P]), sb("zf", [P, P])
        z_hi, z_lo = sb("z_hi", [P, 2, KC, P], F32R), sb("z_lo", [P, 2, KC, P], F32R)
        s_ps, t_ps, z_ps, m_ps = (ps(n, [P, banks, 512]) for n, banks in (("s_ps", RING), ("t_ps", 2), ("z_ps", 1), ("m_ps", 2)))

        w_in, c_in, wh_done, wl_done, c_done = [sem("w_in0"), sem("w_in1")], sem("c_in"), sem("wh_done"), sem("wl_done"), sem("c_done")
        xs_in, xr_in, own = sem("xs_in"), sem("xr_in"), sem("own")
        xn_ready, x_hi_done = sem("xn_ready"), sem("x_hi_done")
        m_ready, m_done = [sem("m0_ready"), sem("m1_ready")], [sem("m0_done"), sem("m1_done")]
        q_hi_done, kf_hi_done, k_done = sem("q_hi_done"), sem("kf_hi_done"), sem("k_done")
        r_f_ready, r_hi_done, r_lo_done = sem("r_f_ready"), sem("r_hi_done"), sem("r_lo_done")
        s_ready, mx_ready, p_ready, t_ready = (sem(n) for n in ("s_ready", "mx_ready", "p_ready", "t_ready"))
        pt_act, pt_dve, pv_ready, inv_ready, wide_ready = (sem(n) for n in ("pt_act", "pt_dve", "pv_ready", "inv_ready", "wide_ready"))
        gp_own = sem("gp_own")
        zf_ready, z_hi_done, z_lo_done, y_ready, stored = (sem(n) for n in ("zf_ready", "z_hi_done", "z_lo_done", "y_ready", "stored"))

        xv = x_in.rearrange("(b t p) d -> b p t d", t=GT, p=P)
        ov = x_out.rearrange("(b t p) d -> b p t d", t=GT, p=P)
        ident = const[:, C_ID:C_ID + P]
        block = ctx.enter_context(nc.Block())

        JOBS = {0: [("x", 3)], 1: [("q1", 3)], 2: [("q2", 3), ("k1", 5)], 3: [("k2", 3), ("v1", 5)], 4: [("v2", 3)]}
        PREPARE = ["x", "q1", "q2", "k1", "k2", "v1", "v2"]
        ORDER = ([], [])
        for o in range(OCT):
            ORDER[0].append(("r", o))
            for kind, _ in JOBS.get(o, []):
                ORDER[0].append((kind, 0))
                ORDER[1].append((kind, 0))
            if o % 2 == 0:
                ORDER[1].append(("o", o))
        MISSING = (("r", 0), ("o", 0))

        def number(bank, kind, o, b, last_one=False):
            if b is None:
                return PREPARE.index(kind)
            at = ORDER[bank].index((kind, o if kind in "ro" else 0))
            n = len(PREPARE) + at - 1
            if isinstance(b, int) and b == 0 and at < ORDER[bank].index(MISSING[bank]):
                n += 1
            if last_one:
                n -= sum(kind_ in PREPARE for kind_, _ in ORDER[bank][:at])
            return b * len(ORDER[bank]) + n

        def number_end(bank):
            return len(PREPARE) - 1 + BATCH * len(ORDER[bank]) - len(PREPARE)

        def slot(o, j):
            u = o * UNIT + j
            before = u - RING if u >= RING else max(w for w in range(-OCT * UNIT, 0) if w % (OCT * UNIT) % RING == u % RING)
            return u % RING, before

        def wait_slot(eng, count, octet, o, j):
            before = slot(o, j)[1]
            if not isinstance(octet, int) or (octet - o) * UNIT + before >= 0:
                eng.wait_ge(count, octet * UNIT + (before - o * UNIT + 1))

        def wait_evac(eng, octet, j):
            eng.wait_ge(pt_dve if j % 2 else pt_act, octet * (UNIT // 2) + (j // 2 + 1))

        def evac(eng, octet, o, j, copy, done):
            eng.wait_ge(t_ready, octet * UNIT + (j + 1))
            if j < 2 and (not isinstance(octet, int) or octet > 1):
                eng.wait_ge(pv_ready, octet - 1)
            kw = (o // 2 + 1) * P
            copy(pt[:, o % 2, j, 0:o // 2 + 1], t_ps[:, j % 2, 0:kw].rearrange("p (k q) -> p k q", q=P)).then_inc(done, 1)

        def walk(b, first, last_one, ahead, main, extra):
            for o in range(OCT):
                octet = b * OCT + o
                has_next = not (last_one and o == OCT - 1)
                has_prev = not (first and o == 0)
                for j in range(UNIT):
                    if j + AHEAD < UNIT:
                        ahead(octet, o, j + AHEAD)
                    elif has_next:
                        ahead(octet + 1, (o + 1) % OCT, j + AHEAD - UNIT, o + 1 == OCT)
                    main(octet, o, j)
                    extra(octet, o, j, has_prev)

        def over_batches(eng, batch, prepare=None, each=lambda b: None):
            batch(0, 0, True, False)
            with eng.Fori(0, BATCH // 2 - 1) as i:
                each(i)
                batch(i * 2 + 1, 1, False, False)
                batch(i * 2 + 2, 0, False, False)
            each(BATCH // 2 - 1)
            batch(BATCH - 1, 1, False, True)

        @block.sync
        def _(sp):
            views = [w.rearrange("(k p) c -> p k c", p=P) for w in (wq, wk, wv, wqi, wki, wvi, wo)]
            sp.dma_start(xs[:], xv[0]).then_inc(xs_in, 16)
            for n, view in enumerate(views):
                if n >= 2:
                    sp.wait_ge(wl_done, n - 1)
                sp.dma_start(raw[:, n % 2].rearrange("p (k c) -> p k c", k=KC), view).then_inc(w_in[n % 2], 16)
                if n == 1:
                    sp.dma_start(bias[:], b_in).then_inc(c_in, 16)
                    sp.dma_start(rows_b[:], b_row.rearrange("(o n) d -> o n d", o=1).to_broadcast([P, 2, D])).then_inc(c_in, 16)
                    sp.dma_start(cos[:], rope[0]).then_inc(c_in, 16)
                    sp.dma_start(sin[:], rope[1]).then_inc(c_in, 16)
                    sp.dma_start(mask_f[:], mask[:, 0:P]).then_inc(c_in, 16)
                    sp.dma_start(even_odd[:], mask[:, P:P + 2]).then_inc(c_in, 16)
            for b in range(BATCH):
                if b + 1 < BATCH:
                    sp.wait_ge(xn_ready, b + 1)
                    sp.dma_start(xs[:], xv[b + 1]).then_inc(xs_in, 16)
                if b:
                    sp.wait_ge(y_ready, b * GT)
                    sp.dma_start(ov[b - 1], y[:]).then_inc(stored, 16)
                sp.dma_start(x_res[:], xv[b]).then_inc(xr_in, 16)
            sp.wait_ge(y_ready, BATCH * GT)
            sp.dma_start(ov[BATCH - 1], y[:]).then_inc(stored, 16)
            sp.wait_ge(stored, 16 * BATCH)

        @block.tensor
        def _(pe):
            def take(bank, kind, o, b, last_one=False):
                n = number(bank, kind, o, b, last_one) if o != "end" else number_end(bank)
                if not isinstance(n, int) or n > 0:
                    pe.wait_ge(m_done[bank], n)
                return m_ps[:, bank]

            def job(kind, o, b, batch):
                if kind == "x":
                    pe.wait_ge(xn_ready, batch + 1)
                elif kind in ("q2", "k2", "v2"):
                    pe.wait_ge(r_lo_done, batch * 3 + ("q2", "k2", "v2").index(kind) + 1)
                for m in range(2):
                    out = take(m, kind, o, b)
                    if kind == "q1" and m == 0:
                        pe.wait_ge(m_done[1], number(1, "x", o, b) + 1)
                    if kind == "x":
                        for t in range(GT):
                            last = pe.transpose(out[:, t * P:(t + 1) * P], xn[:, t, m * P:(m + 1) * P], ident)
                    elif kind == "v2":
                        for t in range(2):
                            cols = slice((2 * m + t) * P, (2 * m + t + 1) * P)
                            for k in range(KC):
                                last = mm3(pe, out[:, t * D:(t + 1) * D], r_hi[:, k, cols], r_lo[:, k, cols],
                                           w_hi[:, 5, k * D:(k + 1) * D], w_lo[:, 5, k * D:(k + 1) * D], k == 0, k == KC - 1)
                    else:
                        w = "qkv".index(kind[0]) + (3 if kind[1] == "2" else 0)
                        hi, lo = (x_hi, x_lo) if kind[1] == "1" else (r_hi, r_lo)
                        for k in range(KC):
                            c = k * D + m * P
                            last = mm3(pe, out, w_hi[:, w, c:c + P], w_lo[:, w, c:c + P], hi[:, k], lo[:, k], k == 0, k == KC - 1)
                    last.then_inc(m_ready[m], 1)

            def batch(b, buf, first, last_one):
                def scores(octet, o, j, following=False):
                    sb_ = 1 - buf if following else buf
                    if o == 0 and j == 0:
                        pe.wait_ge(k_done, (b + (2 if following else 1)) * 4)
                        if following:
                            pe.wait_ge(m_done[0], number(0, "v2", 0, b) + 1)
                            pe.wait_ge(m_done[1], number(1, "v2", 0, b) + 1)
                        else:
                            pe.wait_ge(m_done[0], len(PREPARE))
                            pe.wait_ge(m_done[1], len(PREPARE))
                    wait_slot(pe, p_ready, octet, o, j)
                    qt, c, odd, g = o // 2, o % 2, j // 4, j % 4
                    kw = (qt + 1) * P
                    rows, cols = slice(32 * g, 32 * g + 32), slice(qt * P, kw)
                    out = s_ps[:, slot(o, j)[0]]
                    mm3(pe, out[:, 0:kw], q_hi[rows, sb_, c, cols], q_lo[rows, sb_, c, cols], k_hi[rows, sb_, odd, c, 0:kw],
                        k_lo[rows, sb_, odd, c, 0:kw], True, False)
                    pe.matmul(out[:, kw - P:kw], ident_b[:], mask_b[:], start=False, stop=True,
                              skip_group_check=True).then_inc(s_ready, 1)

                def turn_p(octet, o, j):
                    pe.wait_ge(p_ready, octet * UNIT + (j + 1))
                    if not isinstance(octet, int) or octet * UNIT + j >= 2:
                        before = (octet, j - 2) if j >= 2 else (octet - 1, j - 2 + UNIT)
                        wait_evac(pe, *before)
                    for kt in range(o // 2 + 1):
                        last = pe.transpose(t_ps[:, j % 2, kt * P:(kt + 1) * P], prob[:, slot(o, j)[0], kt * P:(kt + 1) * P], ident)
                    last.then_inc(t_ready, 1)

                def extra(octet, o, j, has_prev):
                    if j == 1 and has_prev:
                        values(octet - 1, (o - 1) % OCT, 1 - buf if o == 0 else buf)
                    if j == 2 and has_prev:
                        spread_sums(octet - 1, o, b)
                    if not last_one:
                        for kind, at in JOBS.get(o, []):
                            if at == j:
                                job(kind, o, b, b + 1)
                    if j == 7 and o % 2 == 0 and has_prev:
                        output(octet - 1, (o // 2 - 1) % QT, o, b)

                def spread_sums(octet, o, b):
                    pe.wait_ge(wide_ready, octet + 1)
                    out = take(0, "r", o, b, last_one)
                    pe.transpose(out[:, 0:P], wide[:, (o - 1) % 2], ident).then_inc(m_ready[0], 1)

                def output(octet, tile, o, b):
                    pe.wait_ge(z_lo_done, octet + 1)
                    out_product(take(1, "o", o, b, last_one), tile)

                if first:
                    for j in range(AHEAD):
                        scores(0, 0, j)
                walk(b, first, last_one, scores, turn_p, extra)

            def values(octet, o, buf):
                wait_evac(pe, octet, UNIT - 1)
                wait_evac(pe, octet, UNIT - 2)
                if not isinstance(octet, int) or octet >= 1:
                    pe.wait_ge(zf_ready, octet)
                qt, c = o // 2, o % 2
                for odd in range(2):
                    for kt in range(qt + 1):
                        for g in range(4):
                            last = pe.matmul(z_ps[32 * g:32 * g + 32, 0, 0:P], v[:, buf, kt, 4 * c + g, odd],
                                             pt[:, o % 2, 4 * odd + g, kt], start=(odd == 0 and kt == 0),
                                             stop=(odd == 1 and kt == qt), skip_group_check=True)
                last.then_inc(pv_ready, 1)

            def out_product(out, tile):
                for c in range(KC):
                    last = mm3(pe, out[:, 0:D], z_hi[:, tile % 2, c], z_lo[:, tile % 2, c],
                               w_hi[:, 6, c * D:(c + 1) * D], w_lo[:, 6, c * D:(c + 1) * D], c == 0, c == KC - 1)
                last.then_inc(m_ready[1], 1)

            pe.wait_ge(wl_done, NW)
            pe.wait_ge(c_done, 3)
            for kind in PREPARE:
                job(kind, None, None, 0)
            over_batches(pe, batch)
            end = BATCH * OCT - 1
            values(end, OCT - 1, 1)
            pe.wait_ge(wide_ready, end + 1)
            pe.transpose(take(0, "r", "end", BATCH)[:, 0:P], wide[:, 1], ident).then_inc(m_ready[0], 1)
            pe.wait_ge(z_lo_done, end + 1)
            out_product(take(1, "o", "end", BATCH), QT - 1)

        @block.scalar
        def _(act):
            def copy(out, in_, done, **more):
                act.activation(out, in_, ACT.Copy, **more).then_inc(done, 1)

            def job(kind, o, b, batch, buf):
                if kind in ("q1", "k1", "v1"):
                    n = batch * 3 + "qkv".index(kind[0])
                    act.wait_ge(r_f_ready, n + 1)
                    copy(r_hi[:], r_f[:], r_hi_done)
                    return
                if kind == "v2":
                    return
                for m in range(2):
                    act.wait_ge(m_ready[m], number(m, kind, o, b) + 1)
                    if kind == "x":
                        copy(x_hi[:, m], m_ps[:, m], x_hi_done)
                    elif kind == "q2":
                        act.activation(q_hi[:, buf, m], m_ps[:, m], ACT.Identity, bias=bias[:, 0, m:m + 1]).then_inc(q_hi_done, 1)
                    elif kind == "k2":
                        act.activation(kf_hi[:, m], m_ps[:, m], ACT.Identity, bias=bias[:, 1, m:m + 1]).then_inc(kf_hi_done, 1)

            def batch(b, buf, first, last_one):
                def exp(octet, o, j, following=False):
                    act.wait_ge(mx_ready, octet * UNIT + (j + 1))
                    wait_slot(act, t_ready, octet, o, j)
                    if j == 0 and (not isinstance(octet, int) or octet >= 2):
                        act.wait_ge(inv_ready, octet - 1)
                    at, kw = slot(o, j)[0], (o // 2 + 1) * P
                    act.activation(prob[:, at, 0:kw], s_ps[:, at, 0:kw], ACT.Exp, bias=nmx[:, at:at + 1], scale=SCALE,
                                   accum_out=sums[:, o % 2, j:j + 1]).then_inc(p_ready, 1)

                def main(octet, o, j):
                    if j % 2 == 0:
                        evac(act, octet, o, j, lambda out, in_: act.activation(out, in_, ACT.Copy), pt_act)

                def extra(octet, o, j, has_prev):
                    if j == 3 and has_prev:
                        sums_out(octet - 1, number(0, "r", o, b, last_one))
                    if j == 5 and has_prev:
                        z_hi_part(octet - 1, (o - 1) % OCT)
                    if not last_one:
                        for kind, at in JOBS.get(o, []):
                            if at + 1 == j and not kind.endswith("1"):
                                job(kind, o, b, b + 1, 1 - buf)
                        for kind, _ in JOBS.get(o - 1, []):
                            if kind.endswith("1") and j == 1:
                                job(kind, o, b, b + 1, 1 - buf)

                if first:
                    for j in range(AHEAD):
                        exp(0, 0, j)
                walk(b, first, last_one, exp, main, extra)

            def sums_out(octet, n):
                act.wait_ge(m_ready[0], n + 1)
                if not isinstance(octet, int) or octet > 0:
                    act.wait_ge(zf_ready, octet)
                copy(rt[:], m_ps[:, 0, 0:P], m_done[0])

            def z_hi_part(octet, o):
                act.wait_ge(zf_ready, octet + 1)
                copy(z_hi[:, (o // 2) % 2, o % 2], zf[:], z_hi_done)

            act.wait_ge(c_in, 96)
            copy(ident_b[:], ident, c_done)
            copy(mask_b[:], mask_f[:], c_done)
            for n in range(NW):
                act.wait_ge(w_in[n % 2], 16 * (n // 2 + 1))
                copy(w_hi[:, n], raw[:, n % 2], wh_done)
            for kind in PREPARE:
                job(kind, None, None, 0, 0)
            over_batches(act, batch)
            end = BATCH * OCT - 1
            sums_out(end, number_end(0))
            z_hi_part(end, OCT - 1)

        @block.gpsimd
        def _(gp):
            one = const[:, C_POW:C_POW + 1].to_broadcast([P, P])

            def rotate(n, kind, o, b):
                for m in range(2):
                    gp.wait_ge(m_done[m], number(m, kind, o, b) + 1)
                if not isinstance(n, int) or n > 0:
                    gp.wait_ge(r_hi_done, n)
                gp.tensor_tensor(r_f[:, 0], turn[:, 0], turn[:, 1], ALU.add).then_inc(gp_own, 1)
                gp.tensor_tensor(r_f[:, 1], turn[:, 2], turn[:, 3], ALU.subtract).then_inc(r_f_ready, 1)

            def rotate_lo(n):
                gp.wait_ge(r_hi_done, n + 1)
                gp.tensor_tensor(r_lo[:], r_f[:], r_hi[:].bitcast(F32), ALU.subtract).then_inc(r_lo_done, 1)

            def keys(batch, buf, b):
                for m in range(2):
                    gp.wait_ge(m_done[m], number(m, "k2", 0, b) + 1)
                for odd in range(2):
                    m = even_odd[:, odd:odd + 1].unsqueeze(2).to_broadcast([P, KC, SEQ])
                    gp.tensor_tensor(k_hi[:, buf, odd], kf_hi[:].bitcast(F32), m, ALU.mult).then_inc(k_done, 1)
                    gp.tensor_tensor(k_lo[:, buf, odd], kf_lo[:].bitcast(F32), m, ALU.mult).then_inc(k_done, 1)

            def batch(b, buf, first, last_one):
                def extra(octet, o, j, has_prev):
                    if j == 1 and has_prev:
                        widen(octet - 1, (o - 1) % 2)
                    if j == 7 and not last_one and any(kind.endswith("1") for kind, _ in JOBS.get(o, [])):
                        rotate((b + 1) * 3 + (o - 1), ("q1", "k1", "v1")[o - 1], o, b)
                    if not last_one and j == 2 and o in (2, 3, 4):
                        rotate_lo((b + 1) * 3 + (o - 2))
                    if not last_one and j == 4 and o == 3:
                        keys(b + 1, 1 - buf, b)
                    if j == 0 and o % 2 == 1 and (not first or o > 1):
                        add_bias(b, o // 2 - 1, number(1, "o", o - 1, b, last_one))
                walk(b, first, last_one, lambda *a: None, lambda *a: None, extra)

            def widen(octet, at):
                gp.wait_ge(inv_ready, octet + 1)
                each = inv[:, at].rearrange("p (odd g) -> p g odd", odd=2).unsqueeze(3).to_broadcast([P, 4, 2, DK0])
                gp.tensor_tensor(wide[:, at].rearrange("p (g odd i) -> p g odd i", g=4, odd=2), each,
                                 one.rearrange("p (g odd i) -> p g odd i", g=4, odd=2), ALU.mult).then_inc(wide_ready, 1)

            def add_bias(b, tile, n):
                gp.wait_ge(m_done[1], n + 1)
                at = tile % GT
                gp.tensor_tensor(y[:, at], y[:, at], rows_b[:, 1], ALU.add).then_inc(y_ready, 1)

            for n, kind in enumerate(("q1", "k1", "v1")):
                rotate(n, kind, None, None)
                rotate_lo(n)
                if n == 1:
                    keys(0, 0, None)
            over_batches(gp, batch)
            widen(BATCH * OCT - 1, 1)
            add_bias(BATCH, -1, number_end(1))

        @block.vector
        def _(dve):
            st = Steps(dve, own)

            def lo(out, in_, hi, done):
                dve.tensor_tensor(out, in_, hi.bitcast(F32), ALU.subtract).then_inc(done, 1)

            def normalise(batch):
                row_stats(dve, st, lambda g: dve.wait_ge(xs_in, batch * 16 + 16), xs, stats, mean, var, rstd, tmp, half)
                for t in range(GT):
                    last = dve.tensor_scalar(xn[:, t], xs[:, t], mean[:, t:t + 1], rstd[:, t:t + 1], ALU.subtract, ALU.mult)
                last.then_inc(xn_ready, 1)

            def job(kind, o, b, batch, buf):
                if kind == "x":
                    for m in range(2):
                        dve.wait_ge(x_hi_done, batch * 2 + (m + 1))
                        lo(x_lo[:, m], m_ps[:, m], x_hi[:, m], m_done[m])
                elif kind.endswith("1"):
                    n = batch * 3 + "qkv".index(kind[0])
                    if not isinstance(n, int) or n > 0:
                        dve.wait_ge(r_f_ready, n)
                    for m in range(2):
                        dve.wait_ge(m_ready[m], number(m, kind, o, b) + 1)
                        dve.tensor_tensor(turn[:, 2 * m], m_ps[:, m], cos[:], ALU.mult)
                        dve.tensor_tensor(turn[:, 3 - 2 * m], m_ps[:, m], sin[:], ALU.mult).then_inc(m_done[m], 1)
                elif kind in ("q2", "k2"):
                    w = "qk".index(kind[0])
                    for m in range(2):
                        dve.wait_ge(q_hi_done if w == 0 else kf_hi_done, batch * 2 + (m + 1))
                        if w and m == 0 and (not isinstance(batch, int) or batch > 0):
                            dve.wait_ge(k_done, batch * 4)
                        out, hi = (q_lo[:, buf, m], q_hi[:, buf, m]) if w == 0 else (kf_lo[:, m], kf_hi[:, m])
                        dve.scalar_tensor_tensor(out, m_ps[:, m], bias[:, w, m:m + 1], hi.bitcast(F32), ALU.add,
                                                 ALU.subtract).then_inc(m_done[m], 1)
                else:
                    for m in range(2):
                        dve.wait_ge(m_ready[m], number(m, kind, o, b) + 1)
                        for t in range(2):
                            kt = 2 * m + t
                            place = v[:, buf, kt].rearrange("p h o i -> p h (o i)")
                            for odd in range(2):
                                src = m_ps[:, m, t * D:(t + 1) * D].rearrange("p (h o i) -> p h o i", o=2, i=DK0)[:, :, odd]
                                row = rows_b[:, 0].rearrange("p (h o i) -> p h o i", o=2, i=DK0)[:, :, odd]
                                last = dve.tensor_tensor(place[:, :, odd * 48:odd * 48 + DK0], src, row, ALU.add)
                        last.then_inc(m_done[m], 1)

            def z_out(octet, n):
                dve.wait_ge(m_done[0], n + 1)
                dve.wait_ge(pv_ready, octet + 1)
                if not isinstance(octet, int) or octet > 0:
                    dve.wait_ge(z_hi_done, octet)
                dve.tensor_tensor(zf[:], z_ps[:, 0, 0:P], rt[:], ALU.mult).then_inc(zf_ready, 1)

            def z_lo_part(octet, o):
                dve.wait_ge(z_hi_done, octet + 1)
                lo(z_lo[:, (o // 2) % 2, o % 2], zf[:], z_hi[:, (o // 2) % 2, o % 2], z_lo_done)

            def invert(octet, at):
                dve.wait_ge(p_ready, octet * UNIT + UNIT)
                dve.reciprocal(inv[:, at], sums[:, at]).then_inc(inv_ready, 1)

            def residual(b, tile, n):
                dve.wait_ge(m_ready[1], n + 1)
                if tile == 0:
                    dve.wait_ge(xr_in, b * 16 + 16)
                    if not isinstance(b, int) or b > 0:
                        dve.wait_ge(stored, b * 16)
                at = tile % GT
                dve.tensor_tensor(y[:, at], m_ps[:, 1, 0:D], x_res[:, at], ALU.add).then_inc(m_done[1], 1)

            def batch(b, buf, first, last_one):
                def maximum(octet, o, j, following=False):
                    dve.wait_ge(s_ready, octet * UNIT + (j + 1))
                    wait_slot(dve, p_ready, octet, o, j)
                    at, kw = slot(o, j)[0], (o // 2 + 1) * P
                    st.link(dve.tensor_reduce(mx[:, at:at + 1], s_ps[:, at, 0:kw], AX.X, ALU.max))
                    dve.tensor_scalar(nmx[:, at:at + 1], mx[:, at:at + 1], -SCALE, None, ALU.mult).then_inc(mx_ready, 1)

                def main(octet, o, j):
                    if j % 2:
                        evac(dve, octet, o, j, dve.tensor_copy, pt_dve)

                def extra(octet, o, j, has_prev):
                    if j == 0 and has_prev:
                        invert(octet - 1, (o - 1) % 2)
                    if j == 4 and has_prev:
                        z_out(octet - 1, number(0, "r", o, b, last_one))
                    if j == 6 and has_prev:
                        z_lo_part(octet - 1, (o - 1) % OCT)
                    if not last_one:
                        if o == 0 and j == 1:
                            normalise(b + 1)
                        for kind, at in JOBS.get(o, []):
                            if at + 1 == j:
                                job(kind, o, b, b + 1, 1 - buf)
                    if j == 7 and o % 2 == 0 and has_prev:
                        residual(b, o // 2 - 1, number(1, "o", o, b, last_one))

                if first:
                    for j in range(AHEAD):
                        maximum(0, 0, j)
                walk(b, first, last_one, maximum, main, extra)

            dve.memset(v[:], 0.0).then_inc(c_done, 1)
            for n in range(NW):
                dve.wait_ge(wh_done, n + 1)
                lo(w_lo[:, n], raw[:, n % 2], w_hi[:, n], wl_done)
            normalise(0)
            dve.wait_ge(c_in, 96)
            dve.wait_ge(c_done, 3)
            for kind in PREPARE:
                job(kind, None, None, 0, 0)
            counted = []

            def counting(b, buf, first, last_one):
                begun = st.n
                batch(b, buf, first, last_one)
                counted.append(st.n - begun)

            def at_top(i):
                if len(counted) == 1:
                    counted.append(st.n)
                per = counted[0] - AHEAD
                st.enter(i * (2 * per) + counted[1])

            over_batches(dve, counting, each=at_top)
            end = BATCH * OCT - 1
            invert(end, 1)
            z_out(end, number_end(0))
            z_lo_part(end, OCT - 1)
            residual(BATCH, -1, number_end(1))


H1, DK1 = 16, 64
PAIRS = H1 // 2
NB1 = PAIRS * UNIT


def attention1(nc, tag, x_in, x_out, wq, wk, wv, wo, const):
    SCALE = DK1 ** -0.5
    with ExitStack() as ctx:
        pool = Pools(nc, ctx, tag)
        sb, ps, sem = pool.sb, pool.ps, pool.sem
        WC = H1 * DK1
        raw = sb("raw", [P, KC * WC])
        w_hi = [sb(f"w{n}_hi", [P, KC * WC], F32R) for n in "qkvo"]
        w_lo = [sb(f"w{n}_lo", [P, KC * WC], F32R) for n in "qkvo"]
        xs, xn, x_sum, y = (sb(n, [P, GT, D]) for n in ("xs", "xn", "x_sum", "y"))
        stats = sb("stats", [P, GT, 6])
        mean, var, rstd, tmp = (sb(n, [P, GT]) for n in ("mean", "var", "rstd", "tmp"))
        half = sb("half", [P, GT], I32)
        x_hi, x_lo = sb("x_hi", [P, KC, SEQ], F32R), sb("x_lo", [P, KC, SEQ], F32R)
        q_hi, q_lo, k_hi, k_lo = (sb(n, [P, 2, SEQ], F32R) for n in ("q_hi", "q_lo", "k_hi", "k_lo"))
        v = sb("v", [P, 2, QT, P])
        mx, nmx = sb("mx", [P, RING]), sb("nmx", [P, RING])
        sums, inv = sb("sums", [P, 2, UNIT]), sb("inv", [P, 2, UNIT])
        prob = sb("prob", [P, RING, SEQ])
        pt = sb("pt", [P, 2, 2, QT, SEQ])
        wide = sb("wide", [P, 2, QT, 2, DK1])
        rt = sb("rt", [P, SEQ])
        zf = sb("zf", [P, SEQ])
        z_hi, z_lo = sb("z_hi", [P, PAIRS, SEQ], F32R), sb("z_lo", [P, PAIRS, SEQ], F32R)
        s_ps, t_ps, z_ps, m_ps = (ps(n, [P, banks, 512]) for n, banks in (("s_ps", RING), ("t_ps", 2), ("z_ps", 1), ("m_ps", 2)))

        w_in, wh_done, wl_done = sem("w_in"), sem("wh_done"), sem("wl_done")
        xs_in, sum_ready, own = sem("xs_in"), sem("sum_ready"), sem("own")
        xn_ready, x_hi_done = sem("xn_ready"), sem("x_hi_done")
        m_ready, m_done = [sem("m0_ready"), sem("m1_ready")], [sem("m0_done"), sem("m1_done")]
        q_hi_done, k_hi_done = sem("q_hi_done"), sem("k_hi_done")
        s_ready, mx_ready, p_ready, t_ready = (sem(n) for n in ("s_ready", "mx_ready", "p_ready", "t_ready"))
        pt_act, pt_dve, pv_ready, inv_ready = (sem(n) for n in ("pt_act", "pt_dve", "pv_ready", "inv_ready"))
        wide_ready, zf_ready, z_hi_done, z_lo_done, stored = (sem(n) for n in ("wide_ready", "zf_ready", "z_hi_done", "z_lo_done", "stored"))

        xv = x_in.rearrange("(b t p) d -> b p t d", t=GT, p=P)
        ov = x_out.rearrange("(b t p) d -> b p t d", t=GT, p=P)
        ident = const[:, C_ID:C_ID + P]
        block = ctx.enter_context(nc.Block())

        ORDER = ([], [])
        for pr in range(PAIRS):
            ORDER[1].append(("r", pr))
            if pr == PAIRS - 1:
                ORDER[0].append(("x", pr))
                ORDER[1].append(("x", pr))
            ORDER[0].extend([("q", pr), ("v", pr)])
            ORDER[1].append(("k", pr))
            if pr == 0:
                ORDER[0].append(("o", pr))
                ORDER[1].append(("o", pr))
        BEFORE = (["x", "q", "v"], ["x", "k"])
        MISSING = ([("o", 0)], [("r", 0), ("o", 0)])

        def number(bank, kind, pr, b):
            if b is None:
                return BEFORE[bank].index(kind)
            if pr == "end":
                after = {"r": 0, "o": bank}[kind]
                return len(BEFORE[bank]) - len(MISSING[bank]) + BATCH * len(ORDER[bank]) - len(BEFORE[bank]) + after
            at = ORDER[bank].index((kind, pr))
            lacks = [ORDER[bank].index(m) for m in MISSING[bank]]
            if isinstance(b, int) and b == 0:
                return len(BEFORE[bank]) + at - sum(m < at for m in lacks)
            return b * len(ORDER[bank]) + (len(BEFORE[bank]) + at - len(lacks))

        def slot(pr, j):
            u = pr * UNIT + j
            before = u - RING if u >= RING else max(w for w in range(-NB1, 0) if w % NB1 % RING == u % RING)
            return u % RING, before

        def wait_slot(eng, sem, pair, pr, j):
            before = slot(pr, j)[1]
            if not isinstance(pair, int) or pair * UNIT + j + before - (pr * UNIT + j) >= 0:
                eng.wait_ge(sem, pair * UNIT + (before - pr * UNIT + 1))

        def evac_of(j):
            on_act = [n for n in range(UNIT) if n % 3 == 0]
            return ("act", on_act.index(j)) if j in on_act else ("dve", j - sum(n < j for n in on_act))
        PER_ACT, PER_DVE = 3, 5

        def wait_evac(eng, pair, j):
            who, n = evac_of(j)
            eng.wait_ge(pt_act if who == "act" else pt_dve, pair * (PER_ACT if who == "act" else PER_DVE) + (n + 1))

        def evac_on(eng, pair, j, buf, copy, done):
            h, qt = divmod(j, QT)
            eng.wait_ge(t_ready, pair * UNIT + (j + 1))
            if j < 3 and (not isinstance(pair, int) or pair > 1):
                eng.wait_ge(pv_ready, pair - 1)
            copy(pt[:, buf, h, :, qt * P:(qt + 1) * P], t_ps[:, j % 2].rearrange("p (k q) -> p k q", k=QT)).then_inc(done, 1)

        @block.sync
        def _(sp):
            views = [w.rearrange("(k p) c -> p k c", p=P) for w in (wq, wk, wv, wo)]
            for n, view in enumerate(views):
                if n:
                    sp.wait_ge(wl_done, n)
                sp.dma_start(raw[:].rearrange("p (k c) -> p k c", k=view.shape[1]), view).then_inc(w_in, 16)
                if n == 0:
                    sp.dma_start(xs[:], xv[0]).then_inc(xs_in, 16)
            for b in range(BATCH):
                if b:
                    sp.wait_ge(m_done[1], number(1, "o", 0, b) + 1)
                    sp.dma_start(ov[b - 1], y[:]).then_inc(stored, 16)
                if b + 1 < BATCH:
                    sp.wait_ge(sum_ready, b + 1)
                    sp.dma_start(xs[:], xv[b + 1]).then_inc(xs_in, 16)
            sp.wait_ge(m_done[1], number(1, "o", "end", BATCH) + 1)
            sp.dma_start(ov[BATCH - 1], y[:]).then_inc(stored, 16)
            sp.wait_ge(stored, 16 * BATCH)

        @block.tensor
        def _(pe):
            def take(bank, kind, pr, b):
                n = number(bank, kind, pr, b)
                if not isinstance(n, int) or n > 0:
                    pe.wait_ge(m_done[bank], n)
                return m_ps[:, bank]

            def transpose_x(pr, b, batch):
                pe.wait_ge(xn_ready, batch + 1)
                for k in range(KC):
                    out = take(k, "x", pr, b)
                    for t in range(GT):
                        last = pe.transpose(out[:, t * P:(t + 1) * P], xn[:, t, k * P:(k + 1) * P], ident)
                    last.then_inc(m_ready[k], 1)

            def project(kind, pair_in_batch, pr, b):
                bank, which = {"q": (0, 0), "k": (1, 1), "v": (0, 2)}[kind]
                if pair_in_batch == 0 and kind == "q":
                    pe.wait_ge(m_done[1], number(1, "x", pr, b) + 1)
                out = take(bank, kind, pr, b)
                if kind == "v":
                    for t in range(QT):
                        for k in range(KC):
                            c = k * WC + pair_in_batch * P
                            last = mm3(pe, out[:, t * P:(t + 1) * P], x_hi[:, k, t * P:(t + 1) * P], x_lo[:, k, t * P:(t + 1) * P],
                                       w_hi[which][:, c:c + P], w_lo[which][:, c:c + P], k == 0, k == KC - 1)
                else:
                    for k in range(KC):
                        c = k * WC + pair_in_batch * P
                        last = mm3(pe, out, w_hi[which][:, c:c + P], w_lo[which][:, c:c + P], x_hi[:, k], x_lo[:, k],
                                   k == 0, k == KC - 1)
                last.then_inc(m_ready[bank], 1)

            def scores(pair, pr, j, buf, job=None):
                if j == 0:
                    pe.wait_ge(m_done[0], number(0, "q", *job) + 1)
                    pe.wait_ge(m_done[1], number(1, "k", *job) + 1)
                pr = pr % PAIRS
                wait_slot(pe, p_ready, pair, pr, j)
                h, qt = divmod(j, QT)
                rows, cols = slice(h * DK1, (h + 1) * DK1), slice(qt * P, (qt + 1) * P)
                mm3(pe, s_ps[:, slot(pr, j)[0]], q_hi[rows, buf, cols], q_lo[rows, buf, cols], k_hi[rows, buf], k_lo[rows, buf],
                    True, True).then_inc(s_ready, 1)

            def transpose_p(pair, pr, j):
                pe.wait_ge(p_ready, pair * UNIT + (j + 1))
                if not isinstance(pair, int) or pair * UNIT + j >= 2:
                    before = (pair, j - 2) if j >= 2 else (pair - 1, j - 2 + UNIT)
                    wait_evac(pe, *before)
                for kt in range(QT):
                    last = pe.transpose(t_ps[:, j % 2, kt * P:(kt + 1) * P], prob[:, slot(pr, j)[0], kt * P:(kt + 1) * P], ident)
                last.then_inc(t_ready, 1)

            def values(pair, part, buf, job):
                if part == 0:
                    for who in ("act", "dve"):
                        wait_evac(pe, pair, max(j for j in range(UNIT) if evac_of(j)[0] == who))
                    pe.wait_ge(m_done[0], number(0, "v", *job) + 1)
                    if not isinstance(pair, int) or pair >= 1:
                        pe.wait_ge(zf_ready, pair)
                for kt in range(part * 2, part * 2 + 2):
                    for h in range(2):
                        rows = slice(h * DK1, (h + 1) * DK1)
                        last = pe.matmul(z_ps[rows, 0], v[:, buf, kt, rows], pt[:, buf, h, kt], start=(kt == 0),
                                         stop=(kt == QT - 1), skip_group_check=True)
                if part:
                    last.then_inc(pv_ready, 1)

            def spread_sums(pair, buf, pr, b):
                pe.wait_ge(wide_ready, pair + 1)
                out = take(1, "r", pr, b)
                for qt in range(QT):
                    last = pe.transpose(out[:, qt * P:(qt + 1) * P], wide[:, buf, qt].rearrange("p h c -> p (h c)"), ident)
                last.then_inc(m_ready[1], 1)

            def outputs(pair, half_, pr, b):
                pe.wait_ge(z_lo_done, pair + 1)
                out = take(half_, "o", pr, b)
                for t in range(2):
                    cols = slice((half_ * 2 + t) * P, (half_ * 2 + t + 1) * P)
                    for c in range(PAIRS):
                        last = mm3(pe, out[:, t * D:(t + 1) * D], z_hi[:, c, cols], z_lo[:, c, cols],
                                   w_hi[3][:, c * D:(c + 1) * D], w_lo[3][:, c * D:(c + 1) * D], c == 0, c == PAIRS - 1)
                last.then_inc(m_ready[half_], 1)

            def job_of(pr, b, first):
                if pr <= 0 and first:
                    return None, None
                return (pr - 1, b) if pr > 0 else (pr - 1 + PAIRS, b - 1)

            def batch(b, first, last_one):
                for pr in range(PAIRS):
                    pair, buf = b * PAIRS + pr, pr % 2
                    has_next = not (last_one and pr == PAIRS - 1)
                    has_prev = not (first and pr == 0)
                    for j in range(UNIT):
                        if j + AHEAD < UNIT:
                            scores(pair, pr, j + AHEAD, buf)
                        elif has_next:
                            scores(pair + 1, pr + 1, j + AHEAD - UNIT, 1 - buf, (pr, b))
                        transpose_p(pair, pr, j)
                        if j == 1 and has_prev:
                            spread_sums(pair - 1, 1 - buf, pr, b)
                        if j in (1, 2) and has_prev:
                            values(pair - 1, j - 1, 1 - buf, job_of(pr - 1, b, first))
                        if pr < PAIRS - 1:
                            if j in (2, 3, 4):
                                project("qkv"[j - 2], pr + 1, pr, b)
                        elif has_next:
                            if j == 2:
                                transpose_x(pr, b, b + 1)
                            if j in (4, 5, 6):
                                project("qkv"[j - 4], 0, pr, b)
                        if pr == 0 and j == 7 and not first:
                            outputs(pair - 1, 0, 0, b)
                        if pr == 1 and j == 0 and not first:
                            outputs(pair - 2, 1, 0, b)

            pe.wait_ge(wl_done, 4)
            transpose_x(None, None, 0)
            for kind in "qkv":
                project(kind, 0, None, None)
            for j in range(AHEAD):
                scores(0, 0, j, 0, (None, None))
            batch(0, True, False)
            with pe.Fori(1, BATCH - 1) as b:
                batch(b, False, False)
            batch(BATCH - 1, False, True)
            end = BATCH * PAIRS - 1
            for part in range(2):
                values(end, part, 1, job_of(PAIRS - 1, BATCH - 1, False))
            spread_sums(end, 1, "end", BATCH)
            for half_ in range(2):
                outputs(end, half_, "end", BATCH)

        @block.scalar
        def _(act):
            def copy(out, in_, done):
                act.activation(out, in_, ACT.Copy).then_inc(done, 1)

            def exp(pair, pr, j, sbuf):
                act.wait_ge(mx_ready, pair * UNIT + (j + 1))
                pr = pr % PAIRS
                wait_slot(act, t_ready, pair, pr, j)
                if j == 0 and (not isinstance(pair, int) or pair >= 2):
                    act.wait_ge(inv_ready, pair - 1)
                at = slot(pr, j)[0]
                act.activation(prob[:, at], s_ps[:, at], ACT.Exp, bias=nmx[:, at:at + 1], scale=SCALE,
                               accum_out=sums[:, sbuf, j:j + 1]).then_inc(p_ready, 1)

            def evac(pair, j, buf):
                if evac_of(j)[0] != "act":
                    return
                evac_on(act, pair, j, buf, lambda o, i: act.activation(o, i, ACT.Copy), pt_act)

            def x_hi_part(pr, b, batch):
                for k in range(KC):
                    act.wait_ge(m_ready[k], number(k, "x", pr, b) + 1)
                    copy(x_hi[:, k], m_ps[:, k], x_hi_done)

            def qk_hi(kind, pair, buf, pr, b):
                bank = 0 if kind == "q" else 1
                act.wait_ge(m_ready[bank], number(bank, kind, pr, b) + 1)
                if kind == "q":
                    copy(q_hi[:, buf], m_ps[:, 0], q_hi_done)
                else:
                    copy(k_hi[:, buf], m_ps[:, 1], k_hi_done)

            def v_out(pair, buf, pr, b):
                act.wait_ge(m_ready[0], number(0, "v", pr, b) + 1)
                if not isinstance(pair, int) or pair >= 2:
                    act.wait_ge(pv_ready, pair - 1)
                last = act.activation(v[:, buf], m_ps[:, 0].rearrange("p (t c) -> p t c", t=QT), ACT.Copy)
                last.then_inc(m_done[0], 1)

            def batch(b, first, last_one):
                for pr in range(PAIRS):
                    pair, buf = b * PAIRS + pr, pr % 2
                    has_next = not (last_one and pr == PAIRS - 1)
                    has_prev = not (first and pr == 0)
                    for j in range(UNIT):
                        if j + AHEAD < UNIT:
                            exp(pair, pr, j + AHEAD, buf)
                        elif has_next:
                            exp(pair + 1, pr + 1, j + AHEAD - UNIT, 1 - buf)
                        evac(pair, j, buf)
                        if j == 2 and has_prev:
                            sums_out(pair - 1, pr, b)
                        if j == 5 and has_prev:
                            if pr == 1 and not first:
                                act.wait_ge(m_ready[1], number(1, "o", 0, b) + 1)
                            z_hi_part(pair - 1, (pr - 1) % PAIRS)
                        if pr < PAIRS - 1:
                            if j in (3, 4):
                                qk_hi("qk"[j - 3], pair + 1, 1 - buf, pr, b)
                            if j == 5:
                                v_out(pair + 1, 1 - buf, pr, b)
                        elif has_next:
                            if j == 3:
                                x_hi_part(pr, b, b + 1)
                            if j == 5:
                                qk_hi("q", pair + 1, 1 - buf, pr, b)
                                qk_hi("k", pair + 1, 1 - buf, pr, b)
                            if j == 7:
                                v_out(pair + 1, 1 - buf, pr, b)

            def sums_out(pair, pr, b):
                act.wait_ge(m_ready[1], number(1, "r", pr, b) + 1)
                if not isinstance(pair, int) or pair > 0:
                    act.wait_ge(zf_ready, pair)
                last = act.activation(rt[:], m_ps[:, 1], ACT.Copy)
                last.then_inc(m_done[1], 1)

            def z_hi_part(pair, c):
                act.wait_ge(zf_ready, pair + 1)
                copy(z_hi[:, c], zf[:], z_hi_done)

            for n in range(4):
                act.wait_ge(w_in, 16 * (n + 1))
                copy(w_hi[n][:], raw[:], wh_done)
            x_hi_part(None, None, 0)
            qk_hi("q", 0, 0, None, None)
            qk_hi("k", 0, 0, None, None)
            v_out(0, 0, None, None)
            for j in range(AHEAD):
                exp(0, 0, j, 0)
            batch(0, True, False)
            with act.Fori(1, BATCH - 1) as b:
                batch(b, False, False)
            batch(BATCH - 1, False, True)
            sums_out(BATCH * PAIRS - 1, "end", BATCH)
            z_hi_part(BATCH * PAIRS - 1, PAIRS - 1)

        @block.gpsimd
        def _(gp):
            one = const[:, C_POW:C_POW + 1].unsqueeze(2).unsqueeze(3).to_broadcast([P, QT, 2, DK1])

            def widen(pair, buf):
                gp.wait_ge(inv_ready, pair + 1)
                each = inv[:, buf].rearrange("p (h t) -> p t h", h=2).unsqueeze(3).to_broadcast([P, QT, 2, DK1])
                gp.tensor_tensor(wide[:, buf], each, one, ALU.mult).then_inc(wide_ready, 1)

            def batch(b, first):
                for pr in range(PAIRS):
                    widen(b * PAIRS + pr, pr % 2)
                    if pr == 1:
                        if not first:
                            for m in range(2):
                                gp.wait_ge(m_done[m], number(m, "o", 0, b) + 1)
                        gp.wait_ge(xn_ready, b + 1)
                        gp.tensor_tensor(x_sum[:], xs[:], xn[:], ALU.add).then_inc(sum_ready, 1)

            batch(0, True)
            with gp.Fori(1, BATCH) as b:
                batch(b, False)

        @block.vector
        def _(dve):
            st = Steps(dve, own)
            NORM = 9 + 16

            def maximum(pair, pr, j):
                dve.wait_ge(s_ready, pair * UNIT + (j + 1))
                pr = pr % PAIRS
                wait_slot(dve, p_ready, pair, pr, j)
                at = slice(slot(pr, j)[0], slot(pr, j)[0] + 1)
                st.link(dve.tensor_reduce(mx[:, at], s_ps[:, slot(pr, j)[0]], AX.X, ALU.max))
                dve.tensor_scalar(nmx[:, at], mx[:, at], -SCALE, None, ALU.mult).then_inc(mx_ready, 1)

            def evac(pair, j, buf):
                if evac_of(j)[0] == "dve":
                    evac_on(dve, pair, j, buf, dve.tensor_copy, pt_dve)

            def normalise(batch):
                row_stats(dve, st, lambda g: dve.wait_ge(xs_in, batch * 16 + 16), xs, stats, mean, var, rstd, tmp, half)
                for t in range(GT):
                    last = dve.tensor_scalar(xn[:, t], xs[:, t], mean[:, t:t + 1], rstd[:, t:t + 1], ALU.subtract, ALU.mult)
                last.then_inc(xn_ready, 1)

            def lo(out, in_, hi, done):
                dve.tensor_tensor(out, in_, hi.bitcast(F32), ALU.subtract).then_inc(done, 1)

            def x_lo_part(batch):
                for k in range(KC):
                    dve.wait_ge(x_hi_done, batch * 2 + (k + 1))
                    lo(x_lo[:, k], m_ps[:, k], x_hi[:, k], m_done[k])

            def qk_lo(kind, pair, buf):
                if kind == "q":
                    dve.wait_ge(q_hi_done, pair + 1)
                    lo(q_lo[:, buf], m_ps[:, 0], q_hi[:, buf], m_done[0])
                else:
                    dve.wait_ge(k_hi_done, pair + 1)
                    lo(k_lo[:, buf], m_ps[:, 1], k_hi[:, buf], m_done[1])

            def invert(pair, buf):
                dve.wait_ge(p_ready, pair * UNIT + UNIT)
                dve.reciprocal(inv[:, buf], sums[:, buf]).then_inc(inv_ready, 1)

            def z_out(pair, buf, pr, b):
                dve.wait_ge(m_done[1], number(1, "r", pr, b) + 1)
                dve.wait_ge(pv_ready, pair + 1)
                if not isinstance(pair, int) or pair > 0:
                    dve.wait_ge(z_hi_done, pair)
                dve.tensor_tensor(zf[:], z_ps[:, 0], rt[:], ALU.mult).then_inc(zf_ready, 1)

            def z_lo_part(pair, c):
                dve.wait_ge(z_hi_done, pair + 1)
                lo(z_lo[:, c], zf[:], z_hi[:, c], z_lo_done)

            def residual(half_, pr, b, batch):
                dve.wait_ge(m_ready[half_], number(half_, "o", pr, b) + 1)
                dve.wait_ge(sum_ready, batch + 1)
                if half_ == 0 and (not isinstance(batch, int) or batch > 0):
                    dve.wait_ge(stored, batch * 16)
                rows = slice(half_ * 2, half_ * 2 + 2)
                last = dve.tensor_tensor(y[:, rows], m_ps[:, half_].rearrange("p (t d) -> p t d", t=2), x_sum[:, rows], ALU.add)
                last.then_inc(m_done[half_], 1)

            def batch(b, first, last_one):
                for pr in range(PAIRS):
                    pair, buf = b * PAIRS + pr, pr % 2
                    has_next = not (last_one and pr == PAIRS - 1)
                    has_prev = not (first and pr == 0)
                    for j in range(UNIT):
                        if j + AHEAD < UNIT:
                            maximum(pair, pr, j + AHEAD)
                        elif has_next:
                            maximum(pair + 1, pr + 1, j + AHEAD - UNIT)
                        evac(pair, j, buf)
                        if j == 0 and has_prev:
                            invert(pair - 1, 1 - buf)
                        if j == 4 and has_prev:
                            z_out(pair - 1, 1 - buf, pr, b)
                        if j == 6 and has_prev:
                            z_lo_part(pair - 1, (pr - 1) % PAIRS)
                        if pr < PAIRS - 1:
                            if j in (3, 4):
                                qk_lo("qk"[j - 3], pair + 1, 1 - buf)
                        elif has_next:
                            if j == 0:
                                normalise(b + 1)
                            if j == 3:
                                x_lo_part(b + 1)
                            if j == 5:
                                qk_lo("q", pair + 1, 1 - buf)
                                qk_lo("k", pair + 1, 1 - buf)
                        if pr == 1 and j < 2 and not first:
                            residual(j, 0, b, b - 1)

            for n in range(4):
                dve.wait_ge(wh_done, n + 1)
                lo(w_lo[n][:], raw[:], w_hi[n][:], wl_done)
            normalise(0)
            x_lo_part(0)
            qk_lo("q", 0, 0)
            qk_lo("k", 0, 0)
            for j in range(AHEAD):
                maximum(0, 0, j)
            start = st.n
            batch(0, True, False)
            per = st.n - start
            with dve.Fori(1, BATCH - 1) as b:
                st.enter(b * per + start)
                batch(b, False, False)
                assert st.n == per
            st.enter((BATCH - 1) * per + start)
            batch(BATCH - 1, False, True)
            end = BATCH * PAIRS - 1
            invert(end, 1)
            z_out(end, 1, "end", BATCH)
            z_lo_part(end, PAIRS - 1)
            for half_ in range(2):
                residual(half_, "end", BATCH, BATCH - 1)




def program(nc, x, wg, w1, b1, w2, b2, wq, wk, wv, wqi, wki, wvi, b_in, b_row, wo, rope, mask,
            gate, m1, m3, m2, aq, ak, av, ao, constants, out):
    hold = [nc.dram_tensor(f"x{n}_dram", (TOK, D), F32, kind="Internal").ap() for n in range(2)]
    rows = nc.dram_tensor("rows_dram", (TOK, ROW), F32, kind="Internal").ap()
    with ExitStack() as ctx:
        const = ctx.enter_context(nc.sbuf_tensor("const", [P, C_END], F32))
        const_in = ctx.enter_context(nc.semaphore("const_in"))
        with nc.Block() as block:
            @block.sync
            def _(sp):
                sp.dma_start(const[:], constants).then_inc(const_in, 16)
                sp.wait_ge(const_in, 16)

        def ffn0(tag, x_in, x_out):
            with ExitStack() as held:
                idx = held.enter_context(nc.sbuf_tensor(f"{tag}_idx", [P, E0, CC], I32))
                ffn0_route(nc, tag + "r", x_in, x_out, rows, wg, const, idx)
                ffn0_experts(nc, tag + "e", rows, x_out, w1, b1, w2, b2, const, idx)

        ffn0("a", x, hold[0])
        attention0(nc, "b", hold[0], hold[1], wq, wk, wv, wqi, wki, wvi, b_in, b_row, wo, rope, mask, const)
        ffn0("c", hold[1], hold[0])
        moe(nc, "d", hold[0], hold[1], gate, m1, m3, m2, const)
        attention1(nc, "e", hold[1], hold[0], aq, ak, av, ao, const)
        moe(nc, "f", hold[0], out, gate, m1, m3, m2, const)


def constants_array():
    c = np.zeros((P, C_END), np.float32)
    p = np.arange(P)
    c[:, C_ID:C_ID + P] = np.eye(P)
    c[:, C_BLK:C_BLK + P] = p[:, None] // SEG == p // SEG
    c[:, C_TRI:C_TRI + P] = (p[:, None] // SEG == p // SEG) & (p[:, None] < p)
    c[:, C_POW:C_POW + C_IOTA - C_POW] = 0.5 ** np.arange(C_IOTA - C_POW)
    c[:, C_IOTA:C_IOTA + P] = p
    c[:, C_PART] = p
    c[:, C_TILE:C_END] = np.arange(C_END - C_TILE)
    return c


def rotation_tables():
    theta = (10000.0 ** (-2.0 * (np.arange(D // 2) - 1.0) / D)).astype(np.float32)
    angle = np.arange(SEQ, dtype=np.float32)[:, None] * theta[None]
    return np.stack([np.cos(angle).T, np.sin(angle).T]).astype(np.float32)


def mask_array():
    p = np.arange(P)
    m = np.zeros((P, P + 2), np.float32)
    m[:, 0:P] = np.where(p[None] > p[:, None], -1e30, 0.0)
    m[:, P] = (p // DK0) % 2 == 0
    m[:, P + 1] = (p // DK0) % 2 == 1
    return m


def kernel(L0_attn_x, L0_attn_wq, L0_attn_wk, L0_attn_wv, L0_attn_in_proj_w, L0_attn_in_proj_b, L0_attn_out_w,
           L0_attn_out_b, L0_ffn_Wg, L0_ffn_W1, L0_ffn_b1, L0_ffn_W2, L0_ffn_b2, L1_attn_w_q, L1_attn_w_k,
           L1_attn_w_v, L1_attn_w_o, L1_ffn_gate_w, L1_ffn_w1, L1_ffn_w2, L1_ffn_w3, L1_ffn_ws1, L1_ffn_ws2,
           L1_ffn_ws3):
    import concourse.bacc as bacc
    from concourse.bass_utils import run_bass_kernel_spmd

    a = np.asarray
    perm = np.concatenate([np.arange(0, D, 2), np.arange(1, D, 2)])
    in_w, in_b = a(L0_attn_in_proj_w), a(L0_attn_in_proj_b)
    heads = lambda w: a(w).transpose(1, 0, 2).reshape(D, -1)
    both = lambda w, s: np.concatenate([a(w), a(s).reshape(D, 2, P).transpose(1, 0, 2)])
    arrays = {
        "x": a(L0_attn_x).reshape(TOK, D),
        "wg": a(L0_ffn_Wg),
        "w1": a(L0_ffn_W1),
        "b1": a(L0_ffn_b1).reshape(E0, FC, P).transpose(0, 2, 1),
        "w2": a(L0_ffn_W2),
        "b2": a(L0_ffn_b2),
        "wq": a(L0_attn_wq).T[:, perm],
        "wk": a(L0_attn_wk).T[:, perm],
        "wv": a(L0_attn_wv).T[:, perm],
        "wqi": in_w[0:D].T[perm],
        "wki": in_w[D:2 * D].T[perm],
        "wvi": in_w[2 * D:3 * D].T[perm],
        "b_in": in_b[:2 * D].reshape(2, KC, P).transpose(2, 0, 1),
        "b_row": np.stack([in_b[2 * D:], a(L0_attn_out_b)]),
        "wo": a(L0_attn_out_w).T,
        "rope": rotation_tables(),
        "mask": mask_array(),
        "gate": a(L1_ffn_gate_w).T,
        "m1": both(L1_ffn_w1, L1_ffn_ws1),
        "m3": both(L1_ffn_w3, L1_ffn_ws3),
        "m2": np.concatenate([a(L1_ffn_w2), a(L1_ffn_ws2).reshape(2, P, D)]),
        "aq": heads(L1_attn_w_q),
        "ak": heads(L1_attn_w_k),
        "av": heads(L1_attn_w_v),
        "ao": a(L1_attn_w_o),
        "constants": constants_array(),
    }
    nc = bacc.Bacc("TRN2", target_bir_lowering=False, num_devices=1)
    given = {f"{name}_dram": np.ascontiguousarray(array) for name, array in arrays.items()}
    taken = {name: nc.dram_tensor(f"{name}_dram", array.shape, F32, kind="ExternalInput").ap() for name, array in arrays.items()}
    out = nc.dram_tensor("out_dram", (TOK, D), F32, kind="ExternalOutput").ap()
    program(nc, out=out, **taken)
    result = run_bass_kernel_spmd(nc, [given], core_ids=[0])
    return result.results[0]["out_dram"].reshape(BATCH, SEQ, D)
```
